# Optimizing a Trainium2 kernel written in Bass

```python
import numpy as np
import jax
import jax.numpy as jnp

def _softmax(x, axis=-1):
    return jax.nn.softmax(x, axis=axis)

def _gelu(x):
    return jax.nn.gelu(x, approximate=True)

def _silu(x):
    return jax.nn.silu(x)

def _sigmoid(x):
    return jax.nn.sigmoid(x)

def _layernorm(x, axis=-1, eps=1e-05):
    m = jnp.mean(x, axis=axis, keepdims=True)
    v = jnp.var(x, axis=axis, keepdims=True)
    return (x - m) / jnp.sqrt(v + eps)

def _scatter_add(tgt, idx, src, axis=0):
    return tgt.at[idx].add(src)

def _segment_sum(src, seg, n):
    return jax.ops.segment_sum(src, seg, n)
kernel_name = 'mk_seq_preln_d2_jaxref_r8_5a2305'

def setup_inputs(seed: int=0):
    np.random.seed(seed)
    _w = jnp.asarray

    def _L0_attn_setup():
        import jax, jax.numpy as jnp
        import numpy as np
        NUM_HEADS = 16
        LAMBDA = 0.1
        HADAMARD_SCALE = 0.05
        ROPE_BASE = 10000.0

        def _rope(t):
            hd = t.shape[-1]
            S = t.shape[2]
            half = hd // 2
            inv_freq = 1.0 / ROPE_BASE ** (jnp.arange(half, dtype=jnp.float32) / half)
            ang = jnp.arange(S, dtype=jnp.float32)[:, None] * inv_freq[None, :]
            cos = jnp.cos(ang).astype(t.dtype)
            sin = jnp.sin(ang).astype(t.dtype)
            t1, t2 = (t[..., :half], t[..., half:])
            return jnp.concatenate([t1 * cos - t2 * sin, t2 * cos + t1 * sin], axis=-1)

        def _rotate_half(t):
            half = t.shape[-1] // 2
            return jnp.concatenate([-t[..., half:], t[..., :half]], axis=-1)
        key = jax.random.key(seed)
        ks = jax.random.split(key, 6)
        B, S, D = (2, 256, 128)
        scale = 1.0 / np.sqrt(D).astype(np.float32)
        x = jax.random.normal(ks[0], (B, S, D), jnp.float32)
        Wq = jax.random.normal(ks[1], (D, D), jnp.float32) * scale
        Wk = jax.random.normal(ks[2], (D, D), jnp.float32) * scale
        Wv = jax.random.normal(ks[3], (D, D), jnp.float32) * scale
        Wo = jax.random.normal(ks[4], (D, D), jnp.float32) * scale
        gate_w = jax.random.normal(ks[5], (D // NUM_HEADS,), jnp.float32) * 0.01
        return {'x': x, 'Wq': Wq, 'Wk': Wk, 'Wv': Wv, 'Wo': Wo, 'gate_w': gate_w}
    _L0_attn_in = _L0_attn_setup()

    def _L0_ffn_setup():
        import jax, jax.numpy as jnp
        import numpy as np
        HIDDEN = 128
        INTER = 512
        key = jax.random.key(seed)
        k1, k2, k3, k4, k5 = jax.random.split(key, 5)
        hidden_states = jax.random.normal(k1, (4, 256, HIDDEN), dtype=jnp.float32)
        W1 = jax.random.normal(k2, (HIDDEN, INTER), dtype=jnp.float32) * (1.0 / np.sqrt(HIDDEN))
        b1 = jax.random.normal(k3, (INTER,), dtype=jnp.float32) * 0.02
        W2 = jax.random.normal(k4, (INTER, HIDDEN), dtype=jnp.float32) * (1.0 / np.sqrt(INTER))
        b2 = jax.random.normal(k5, (HIDDEN,), dtype=jnp.float32) * 0.02
        return {'hidden_states': hidden_states, 'W1': W1, 'b1': b1, 'W2': W2, 'b2': b2}
    _L0_ffn_in = _L0_ffn_setup()

    def _L1_attn_setup():
        import jax, jax.numpy as jnp
        import numpy as np
        import math
        H = 16
        EPS = 1e-05
        key = jax.random.key(seed)
        ks = jax.random.split(key, 4)
        B, T, D = (2, 256, 128)
        s = 1.0 / math.sqrt(D)
        return {'x': jax.random.normal(ks[0], (B, T, D), dtype=jnp.float32), 'ln_g': jnp.ones((D,), jnp.float32), 'ln_b': jnp.zeros((D,), jnp.float32), 'Wq': jax.random.normal(ks[1], (D, D), jnp.float32) * s, 'bq': jnp.zeros((D,), jnp.float32), 'Wk': jax.random.normal(ks[2], (D, D), jnp.float32) * s, 'bk': jnp.zeros((D,), jnp.float32), 'Wv': jax.random.normal(ks[3], (D, D), jnp.float32) * s, 'bv': jnp.zeros((D,), jnp.float32)}
    _L1_attn_in = _L1_attn_setup()

    def _L1_ffn_setup():
        import jax, jax.numpy as jnp
        import numpy as np
        DIM = 128
        HIDDEN = 384
        SCALE = 1.0 / 127.0

        def _dequant(w_int, dtype):
            return w_int.astype(dtype) * jnp.asarray(SCALE, dtype)
        key = jax.random.key(seed)
        k_x, k_g, k_u, k_d = jax.random.split(key, 4)
        x = jax.random.normal(k_x, (4, 256, DIM), dtype=jnp.float32)
        w_gate = jax.random.randint(k_g, (HIDDEN, DIM), -127, 128, dtype=jnp.int32)
        w_up = jax.random.randint(k_u, (HIDDEN, DIM), -127, 128, dtype=jnp.int32)
        w_down = jax.random.randint(k_d, (DIM, HIDDEN), -127, 128, dtype=jnp.int32)
        return {'x': x, 'w_gate': w_gate, 'w_up': w_up, 'w_down': w_down}
    _L1_ffn_in = _L1_ffn_setup()
    _d = {'L0_attn_x': _L0_attn_in['x'], 'L0_attn_Wq': _L0_attn_in['Wq'], 'L0_attn_Wk': _L0_attn_in['Wk'], 'L0_attn_Wv': _L0_attn_in['Wv'], 'L0_attn_Wo': _L0_attn_in['Wo'], 'L0_attn_gate_w': _L0_attn_in['gate_w'], 'L0_ffn_W1': _L0_ffn_in['W1'], 'L0_ffn_b1': _L0_ffn_in['b1'], 'L0_ffn_W2': _L0_ffn_in['W2'], 'L0_ffn_b2': _L0_ffn_in['b2'], 'L1_attn_ln_g': _L1_attn_in['ln_g'], 'L1_attn_ln_b': _L1_attn_in['ln_b'], 'L1_attn_Wq': _L1_attn_in['Wq'], 'L1_attn_bq': _L1_attn_in['bq'], 'L1_attn_Wk': _L1_attn_in['Wk'], 'L1_attn_bk': _L1_attn_in['bk'], 'L1_attn_Wv': _L1_attn_in['Wv'], 'L1_attn_bv': _L1_attn_in['bv'], 'L1_ffn_w_gate': _L1_ffn_in['w_gate'], 'L1_ffn_w_up': _L1_ffn_in['w_up'], 'L1_ffn_w_down': _L1_ffn_in['w_down']}
    _x0 = _d['L0_attn_x']
    _d['L0_attn_x'] = jax.random.normal(jax.random.fold_in(jax.random.key(seed), 1), (8, 256, 128), dtype=_x0.dtype)
    del _x0
    return _d

def reference(L0_attn_x, L0_attn_Wq, L0_attn_Wk, L0_attn_Wv, L0_attn_Wo, L0_attn_gate_w, L0_ffn_W1, L0_ffn_b1, L0_ffn_W2, L0_ffn_b2, L1_attn_ln_g, L1_attn_ln_b, L1_attn_Wq, L1_attn_bq, L1_attn_Wk, L1_attn_bk, L1_attn_Wv, L1_attn_bv, L1_ffn_w_gate, L1_ffn_w_up, L1_ffn_w_down):

    def _L0_attn_ref(x, Wq, Wk, Wv, Wo, gate_w):
        import jax, jax.numpy as jnp
        import numpy as np
        NUM_HEADS = 16
        LAMBDA = 0.1
        HADAMARD_SCALE = 0.05
        ROPE_BASE = 10000.0

        def _rope(t):
            hd = t.shape[-1]
            S = t.shape[2]
            half = hd // 2
            inv_freq = 1.0 / ROPE_BASE ** (jnp.arange(half, dtype=jnp.float32) / half)
            ang = jnp.arange(S, dtype=jnp.float32)[:, None] * inv_freq[None, :]
            cos = jnp.cos(ang).astype(t.dtype)
            sin = jnp.sin(ang).astype(t.dtype)
            t1, t2 = (t[..., :half], t[..., half:])
            return jnp.concatenate([t1 * cos - t2 * sin, t2 * cos + t1 * sin], axis=-1)

        def _rotate_half(t):
            half = t.shape[-1] // 2
            return jnp.concatenate([-t[..., half:], t[..., :half]], axis=-1)
        B, S, D = x.shape
        H = NUM_HEADS
        hd = D // H

        def heads(W):
            return (x @ W.T).reshape(B, S, H, hd).transpose(0, 2, 1, 3)
        Q = _rope(heads(Wq))
        K = _rope(heads(Wk))
        V = heads(Wv)
        causal = jnp.tril(jnp.ones((S, S), dtype=bool))
        inv_sqrt_d = 1.0 / jnp.sqrt(jnp.asarray(hd, x.dtype))

        def attend(q, k):
            s = (jnp.einsum('bhsd,bhtd->bhst', q, k) + LAMBDA * jnp.einsum('bhsd,bhtd->bhst', q * q, k * k)) * inv_sqrt_d
            s = jnp.where(causal, s, jnp.asarray(-1000000000.0, s.dtype))
            a = jax.nn.softmax(s, axis=-1)
            return jnp.einsum('bhst,bhtd->bhsd', a, V)
        out1 = attend(Q, K)
        out2 = attend(_rotate_half(Q), _rotate_half(K))
        out = 0.5 * (out1 + out2) + HADAMARD_SCALE * (out1 * out2) * gate_w
        out = out.transpose(0, 2, 1, 3).reshape(B, S, D)
        return out @ Wo.T

    def _L0_ffn_ref(hidden_states, W1, b1, W2, b2):
        import jax, jax.numpy as jnp
        import numpy as np
        HIDDEN = 128
        INTER = 512
        h = jax.nn.relu(jnp.einsum('bsh,hi->bsi', hidden_states, W1) + b1)
        return jnp.einsum('bsi,ih->bsh', h, W2) + b2

    def _L1_attn_ref(x, ln_g, ln_b, Wq, bq, Wk, bk, Wv, bv):
        import jax, jax.numpy as jnp
        import numpy as np
        import math
        H = 16
        EPS = 1e-05
        B, T, D = x.shape
        mu = jnp.mean(x, axis=-1, keepdims=True)
        var = jnp.mean(jnp.square(x - mu), axis=-1, keepdims=True)
        xn = (x - mu) * jax.lax.rsqrt(var + EPS) * ln_g + ln_b
        q = (xn @ Wq + bq).reshape(B, T, H, D // H)
        k = (xn @ Wk + bk).reshape(B, T, H, D // H)
        v = (xn @ Wv + bv).reshape(B, T, H, D // H)
        scale = 1.0 / math.sqrt(D // H)
        attn = jnp.einsum('bnhd,bmhd->bnmh', q, k) * scale
        w = jax.nn.softmax(attn, axis=2)
        y = jnp.einsum('bnmh,bmhd->bnhd', w, v).reshape(B, T, D)
        return y

    def _L1_ffn_ref(x, w_gate, w_up, w_down):
        import jax, jax.numpy as jnp
        import numpy as np
        DIM = 128
        HIDDEN = 384
        SCALE = 1.0 / 127.0

        def _dequant(w_int, dtype):
            return w_int.astype(dtype) * jnp.asarray(SCALE, dtype)
        wg = _dequant(w_gate, x.dtype)
        wu = _dequant(w_up, x.dtype)
        wd = _dequant(w_down, x.dtype)
        gate = jnp.einsum('bsd,hd->bsh', x, wg)
        up = jnp.einsum('bsd,hd->bsh', x, wu)
        h = jax.nn.silu(gate) * up
        return jnp.einsum('bsh,dh->bsd', h, wd)
    x = L0_attn_x
    x = x + _L0_attn_ref(_layernorm(x, axis=-1), L0_attn_Wq, L0_attn_Wk, L0_attn_Wv, L0_attn_Wo, L0_attn_gate_w)
    x = x + _L0_ffn_ref(_layernorm(x, axis=-1), L0_ffn_W1, L0_ffn_b1, L0_ffn_W2, L0_ffn_b2)
    x = x + _L1_attn_ref(_layernorm(x, axis=-1), L1_attn_ln_g, L1_attn_ln_b, L1_attn_Wq, L1_attn_bq, L1_attn_Wk, L1_attn_bk, L1_attn_Wv, L1_attn_bv)
    x = x + _L1_ffn_ref(_layernorm(x, axis=-1), L1_ffn_w_gate, L1_ffn_w_up, L1_ffn_w_down)
    return x

_drawn_inputs = setup_inputs


def setup_inputs(seed=0):
    import zlib

    import numpy as np

    out = dict(_drawn_inputs(seed))
    spreads = {'L1_attn_ln_g': (1.0, 0.2),
     'L1_attn_ln_b': (0.0, 0.1),
     'L1_attn_bq': (0.0, 0.56),
     'L1_attn_bk': (0.0, 2.0),
     'L1_attn_bv': (0.0, 0.1)}
    factors = {'L0_attn_gate_w': 200.0, 'L0_ffn_b1': 3.307}
    for name, (base, spread) in spreads.items():
        noise = np.random.default_rng([zlib.crc32(name.encode()), seed]).standard_normal(out[name].shape)
        drawn = base * np.exp(spread * noise) if base else spread * noise
        out[name] = jnp.asarray(drawn.astype(out[name].dtype))
    for name, factor in factors.items():
        out[name] = (out[name] * factor).astype(out[name].dtype)
    return out
```

```python
from contextlib import ExitStack

import numpy as np

import concourse.bass as bass
from concourse import mybir

ALU = mybir.AluOpType
ACT = mybir.ActivationFunctionType
AX = mybir.AxisListType
F32 = mybir.dt.float32
F16 = mybir.dt.float16
BF16 = mybir.dt.bfloat16
I32 = mybir.dt.int32
U32 = mybir.dt.uint32

P = 128
B, S, D = 8, 256, 128
H, HD = 16, 8
TPB = S // P
INTER = 512
NI = INTER // P
HIDDEN = 384
NG = HIDDEN // P
HC = H // 2
LAM = 0.1
HADAMARD = 0.05
EPS = 1e-5
SCALE = 1.0 / 127.0
QSCALE = 1.0 / float(np.sqrt(HD))
MROW = 96
RING = 8


def head_of_slot(s):
    return 2 * (4 * (s // 8) + s % 4) + (s % 8) // 4


def program(nc, x, w0, tab, small, w1, wint, ident, masks, out):
    with ExitStack() as ctx:
        def sb(name, shape, dt=F32):
            return ctx.enter_context(nc.sbuf_tensor(name, shape, dt))

        def sem(name):
            return ctx.enter_context(nc.semaphore(name))

        scr = [nc.dram_tensor("scr0", [B, 2, 4, P, S], F16, kind="Internal").ap(),
               nc.dram_tensor("scr1", [B, 2, 2, P, S], F16, kind="Internal").ap()]
        NS = [4, 2]

        xs = sb("xs", [P, B * TPB, D])
        W0 = sb("W0", [P, 6 * D + INTER + NI * D])
        TAB = sb("TAB", [P, 2, 2 * S])
        SM = sb("SM", [P, 4 * D + NI + 5])
        W1 = sb("W1", [P, 3 * D])
        WI = sb("WI", [P, 3 * HIDDEN], I32)
        IDF = sb("IDF", [P, P])
        MSF = sb("MSF", [P, 3, P])
        MSK = sb("MSK", [P, 3, P], BF16)
        WGU = sb("WGU", [P, 2 * HIDDEN], F16)
        WD = sb("WD", [P, NG, D])
        wq, wrq, wk, wrk, wv, wo = [W0[:, n * D:(n + 1) * D] for n in range(6)]
        wi1 = W0[:, 6 * D:6 * D + INTER]
        wi2 = W0[:, 6 * D + INTER:].rearrange("p (n d) -> p n d", n=NI)
        gate_row, b2_row, bv_row = [SM[:, n * D:(n + 1) * D] for n in range(3)]
        b1_col = SM[:, 4 * D:4 * D + NI]
        g_col, b_col, bq_col, bk_col, bqs_col = [SM[:, 4 * D + NI + n:4 * D + NI + n + 1] for n in range(5)]
        EPSC = sb("EPSC", [P, 2, TPB])
        STAT = sb("STAT", [P, 4, 2, TPB, 6])
        MV = sb("MV", [P, 4, 2, TPB, 2])
        VE = sb("VE", [P, 4, 2, TPB])
        RS = sb("RS", [P, 4, 2, TPB])
        HOLD = sb("HOLD", [P, 1])
        XN = [[sb(f"XN{n}{p}", [P, TPB, D]) for p in range(2)] for n in range(4)]
        XT = [[sb(f"XT{n}{p}", [P, S]) for p in range(2)] for n in range(3)]
        XHL = [sb(f"XHL{p}", [P, 2, S], F16) for p in range(2)]
        TQ = [sb(f"TQ{p}", [P, 2, 2 * S]) for p in range(2)]
        QR = [sb(f"QR{p}", [P, 2, 2, S]) for p in range(2)]
        PR = [sb(f"PR{p}", [P, 2, 4, S], F16) for p in range(2)]
        QR1 = [sb(f"QR1{p}", [P, 2, S]) for p in range(2)]
        PR1 = [sb(f"PR1{p}", [P, 2, 2, S], F16) for p in range(2)]
        VA = sb("VA", [P, B * TPB, D])
        VP = [sb(f"VP{p}", [P, TPB, H * 32]) for p in range(2)]
        QS = [[sb(f"QS{L}{p}", [P, H, S], F16) for p in range(2)] for L in range(2)]
        KS = [[sb(f"KS{L}{p}", [P, H, S], F16) for p in range(2)] for L in range(2)]
        PB = [sb(f"PB{n}", [P, 2 * S]) for n in range(RING)]
        NM = [sb(f"NM{p}", [P, H, 3]) for p in range(2)]
        NMB = [sb(f"NMB{p}", [P, H]) for p in range(2)]
        MT = [[sb(f"MT{p}{c}", [HC, 2, S], F16) for c in range(2)] for p in range(2)]
        OT = [[sb(f"OT{p}{c}", [P, S]) for c in range(2)] for p in range(2)]
        REC = [sb(f"REC{p}", [P, 16, 2]) for p in range(2)]
        Y = [sb(f"Y{p}", [P, TPB * D]) for p in range(2)]
        ZG = [sb(f"ZG{p}", [P, TPB * D]) for p in range(2)]
        Z = [sb(f"Z{p}", [P, TPB * D]) for p in range(2)]
        ZT = [sb(f"ZT{p}", [P, S]) for p in range(2)]
        HR = [TQ[p][:, :, :].rearrange("q a (b t) -> q (a b) t", t=S) for p in range(2)]
        TH = [sb(f"TH{j}", [P, S]) for j in range(NG)]
        GA = [sb(f"GA{j}", [P, S]) for j in range(NG)]
        HG = [QR[p][:, :, :, :].rearrange("q a b t -> q (a b) t")[:, 0:NG] for p in range(2)]

        bank = [ctx.enter_context(nc.psum_tensor(f"bank{n}", [P, 512], F32)) for n in range(8)]
        SB_, TB_, VB_, MISC = bank[0:2], bank[2:5], bank[5], bank[6:8]

        s_x, s_w, s_c, s_w1, s_wi = sem("x_loaded"), sem("w0_loaded"), sem("tables_loaded"), sem("w1_loaded"), sem("wint_loaded")
        s_out = sem("out_stored")
        s_init = [[sem(f"stacks_cleared_{L}{p}") for p in range(2)] for L in range(2)]
        s_vz = sem("v_spread_cleared")
        s_msk = sem("masks_narrowed")
        s_prep = sem("weights_prepared")
        s_dve = sem("dve_chain")
        s_pool = sem("pool_chain")
        s_act = sem("act_chain")
        s_var = [sem(f"variance_{n}") for n in range(4)]
        s_stat = [sem(f"half_stats_{n}") for n in range(4)]
        s_res = [sem(f"stream_{n}") for n in range(3)]
        s_rec = [sem(f"o_reciprocals_{L}") for L in range(2)]
        s_rstd = [sem(f"rstd_{n}") for n in range(4)]
        s_xn = [sem(f"normed_{n}") for n in range(4)]
        s_xtp = [sem(f"normedT_psum_{n}") for n in range(4)]
        s_xt = [sem(f"normedT_{n}") for n in range(4)]
        s_xlo = sem("normedT_lo")
        s_qk = sem("rope_qk_psum")
        s_v = [sem("v_psum_0"), sem("v_psum_1")]
        s_va = [sem("v_stored_0"), sem("v_stored_1")]
        s_mul = sem("rope_products")
        s_rot = sem("rope_sums")
        s_hi = sem("hi_0")
        s_lo = sem("lo_0")
        s_scr = [[sem(f"scratch_{L}{p}") for p in range(2)] for L in range(2)]
        s_qk1 = sem("qk1_psum")
        s_qr1 = sem("qk1_biased")
        s_hi1, s_lo1 = sem("hi_1"), sem("lo_1")
        s_st = [[sem(f"stack_{L}{c}") for c in range(2)] for L in range(2)]
        s_s = [sem(f"scores_{L}") for L in range(2)]
        s_mx = [sem(f"maxima_{L}") for L in range(2)]
        s_mb = sem("maxima_merged")
        s_mt = [sem(f"maxima_rows_psum_{L}") for L in range(2)]
        s_ms = [sem(f"maxima_rows_{L}") for L in range(2)]
        s_mi = [[sem(f"maxima_in_{L}{c}") for c in range(2)] for L in range(2)]
        s_t = [sem(f"shifted_scores_{L}") for L in range(2)]
        s_e = [sem(f"probs_{L}") for L in range(2)]
        s_pv = [sem(f"pv_groups_{L}") for L in range(2)]
        s_vp = [sem(f"v_spread_{L}") for L in range(2)]
        s_o = [sem(f"o_evacuated_{L}") for L in range(2)]
        s_ot = [sem(f"o_tokens_psum_{L}") for L in range(2)]
        s_y = [sem(f"o_normalised_{L}") for L in range(2)]
        s_z = sem("gated")
        s_zp, s_zt = sem("gatedT_psum"), sem("gatedT")
        s_wo = sem("wo_psum")
        s_xb = sem("x_plus_b2")
        s_h, s_hr = sem("ffn0_hidden_psum"), sem("ffn0_hidden")
        s_f = sem("ffn0_psum")
        s_gu, s_th, s_ga, s_hg = sem("gate_up_psum"), sem("tanh"), sem("gate_part"), sem("ffn1_hidden")
        s_dn = sem("ffn1_psum")
        s_xo = sem("x_final")

        block = ctx.enter_context(nc.Block())

        def at(per, b, k):
            return b * per + k

        def xt_(b):
            return xs[:, bass.ds(b * TPB, TPB), :]

        def va_(b):
            return VA[:, bass.ds(b * TPB, TPB), :]

        def pairs(eng, body):
            body(0, True, False)
            with eng.Fori(1, B // 2 - 1) as i:
                body(i, False, False)
            body(B // 2 - 1, False, True)

        def phases(eng, phase):
            def body(i, first, last):
                phase(2 * i, 0, True, not first)
                phase(2 * i + 1, 1, not last, True)
            pairs(eng, body)

        @block.sync
        def _(sp):
            sp.dma_start(xs[:, :, :], x.rearrange("b (t p) d -> p (b t) d", p=P)).then_inc(s_x, 16)
            sp.dma_start(W0[:, :], w0).then_inc(s_w, 16)
            sp.dma_start(IDF[:, :], ident).then_inc(s_c, 16)
            sp.dma_start(TAB[:, :, :], tab).then_inc(s_c, 16)
            sp.dma_start(MSF[:, :, :], masks).then_inc(s_c, 16)
            sp.dma_start(SM[:, :], small).then_inc(s_c, 16)
            sp.dma_start(W1[:, :], w1).then_inc(s_w1, 16)
            sp.dma_start(WI[:, :], wint).then_inc(s_wi, 16)

            def store_parts(i, first, last):
                for p in range(2):
                    b = 2 * i + p
                    for n in range(2):
                        sp.wait_ge(s_lo, at(2, b, n + 1))
                        sp.dma_start(scr[0][bass.ds(b, 1), n].rearrange("o s f t -> f (o s) t"),
                                     PR[p][:, n]).then_inc(s_scr[0][p], 16)
            pairs(sp, store_parts)

            def load_stack(L, b, p, c):
                R = NS[L] * HD
                h = R // 2
                cs = slice(HC * c, HC * (c + 1))
                sq, sk = [scr[L][bass.ds(b, 1), n].rearrange("o s (d h) t -> (o s d) h t", h=H) for n in range(2)]
                for dst, src in ((QS[L][p][0:R, cs], sq[:, cs]), (QS[L][p][R:R + h, cs], sq[0:h, cs]),
                                 (KS[L][p][0:h, cs], sk[0:h, cs]), (KS[L][p][h:h + R, cs], sk[:, cs])):
                    sp.dma_start(dst, src).then_inc(s_st[L][c], 16)

            def load_max(L, b, p, c):
                sp.wait_ge(s_ms[L], at(2, b, c + 1))
                for n in range(2):
                    sp.dma_start(QS[L][p][MROW + n:MROW + n + 1, HC * c:HC * (c + 1), :],
                                 MT[p][c][:, n, :]).then_inc(s_mi[L][c], 16)

            for L in range(2):
                def store1(b, p):
                    sp.wait_ge(s_lo1, at(1, b, 1))
                    for n in range(2):
                        sp.dma_start(scr[1][bass.ds(b, 1), n].rearrange("o s f t -> f (o s) t"),
                                     PR1[p][:, n]).then_inc(s_scr[1][p], 16)

                def store_out(b, p):
                    sp.wait_ge(s_xo, at(1, b, 1))
                    sp.dma_start(out[bass.ds(b, 1)].rearrange("o (t p) d -> p (o t) d", p=P), xt_(b)).then_inc(s_out, 16)

                sp.wait_ge(s_init[L][0], 3)
                sp.wait_ge(s_init[L][1], 3)
                for p in range(2):
                    sp.wait_ge(s_scr[L][p], 16 * B)
                for b in range(2):
                    for c in range(2):
                        if b == 1:
                            sp.wait_ge(s_st[L][c], 64)
                        load_stack(L, b, b, c)
                for c in range(2):
                    load_max(L, 0, 0, c)

                def phase(b, p, scores, tail, more=True):
                    for c in range(2):
                        if more:
                            sp.wait_ge(s_t[L], at(16, b, HC * (c + 1)))
                            load_stack(L, b + 2, p, c)
                        if scores and c == 0:
                            load_max(L, b + 1, 1 - p, c)
                    if tail:
                        (store1 if L == 0 else store_out)(b - 1, 1 - p)
                    if scores:
                        load_max(L, b + 1, 1 - p, 1)

                phase(0, 0, True, False)
                phase(1, 1, True, True)
                with sp.Fori(1, B // 2 - 1) as i:
                    phase(2 * i, 0, True, True)
                    phase(2 * i + 1, 1, True, True)
                phase(B - 2, 0, True, True, more=False)
                phase(B - 1, 1, False, True, more=False)
                (store1 if L == 0 else store_out)(B - 1, 1)
            sp.wait_ge(s_out, 16 * B)

        @block.gpsimd
        def _(pool):
            pool.memset(EPSC[:, 0], EPS).then_inc(s_pool, 1)
            pool.memset(EPSC[:, 1], -0.5).then_inc(s_pool, 1)

            def clear_stack(L, p):
                pool.memset(QS[L][p][:, :, :].bitcast(U32), 0).then_inc(s_init[L][p], 1)
                pool.wait_ge(s_init[L][p], 1)
                pool.memset(KS[L][p][0:MROW].bitcast(U32), 0).then_inc(s_init[L][p], 1)
                pool.wait_ge(s_init[L][p], 2)
                pool.memset(KS[L][p][MROW:P], 1.0).then_inc(s_init[L][p], 1)
                pool.wait_ge(s_init[L][p], 3)
            pool.wait_ge(s_pool, 2)
            clear_stack(0, 1)
            pool.wait_ge(s_vz, 2)
            for p in range(2):
                for e in range(2):
                    ones = VP[p][:, :, :].rearrange("q t (c f r) -> q (t c) f r", f=2, r=32)[:, :, e, 16 + e:17 + e]
                    pool.memset(ones, 1.0).then_inc(s_pool, 1)
            pool.wait_ge(s_pool, 6)

            def rstd(n, b, p):
                chain = s_rstd[n]
                pool.wait_ge(s_var[n], at(1, b, 1))
                pool.tensor_tensor(VE[:, n, p], MV[:, n, p, :, 1], EPSC[:, 0], ALU.add).then_inc(chain, 1)
                pool.wait_ge(chain, at(2, b, 1))
                pool.tensor_tensor(RS[:, n, p], VE[:, n, p], EPSC[:, 1], ALU.pow).then_inc(chain, 1)

            def stage_a(i, first, last):
                for p in range(2):
                    rstd(0, 2 * i + p, p)
                for p in range(2):
                    b = 2 * i + p
                    for n in range(2):
                        pool.wait_ge(s_mul, at(2, b, n + 1))
                        pool.tensor_tensor(QR[p][:, n, 0], TQ[p][:, n, 0:S], TQ[p][:, n, S:2 * S],
                                           ALU.add).then_inc(s_rot, 1)
            pairs(pool, stage_a)
            clear_stack(1, 0)
            clear_stack(1, 1)

            def spread_v(L, b, p):
                pool.wait_ge(s_va[L], at(1, b, 1))
                dst = VP[p][:, :, :].rearrange("q t (c r) -> q t c r", r=64)
                for e in range(2):
                    ins = pool.tensor_copy(dst[:, :, :, 40 * e:40 * e + 8],
                                           va_(b).rearrange("q t (c f d) -> q t c f d", f=2, d=HD)[:, :, :, e])
                ins.then_inc(s_vp[L], 1)

            for L in range(2):
                if L == 1:
                    pool.wait_ge(s_pv[0], 4 * B)
                for b in range(2):
                    spread_v(L, b, b)

                def tail_c(c, p):
                    pool.wait_ge(s_y[0], at(1, c, 1))
                    gb = gate_row.rearrange("q (o d) -> q o d", o=1).to_broadcast([P, TPB, D])
                    yv = Y[p][:, :].rearrange("q (t d) -> q t d", t=TPB)
                    pool.tensor_tensor(ZG[p][:, :].rearrange("q (t d) -> q t d", t=TPB), yv, gb, ALU.mult).then_inc(s_z, 1)
                    rstd(1, c, p)
                    pool.wait_ge(s_xn[1], at(1, c, 1))
                    b2 = b2_row.rearrange("q (o d) -> q o d", o=1).to_broadcast([P, TPB, D])
                    pool.tensor_tensor(xt_(c), xt_(c), b2, ALU.add).then_inc(s_xb, 1)
                    rstd(2, c, p)
                    pool.wait_ge(s_hi1, at(1, c, 1))
                    pool.tensor_tensor(PR1[p][:, :, 1], QR1[p][:, :, :], PR1[p][:, :, 0], ALU.subtract).then_inc(s_lo1, 1)

                def tail_e(c, p):
                    rstd(3, c, p)

                tail = tail_e if L else tail_c

                def phase(b, p, scores, with_tail, more=True):
                    if with_tail:
                        tail(b - 1, 1 - p)
                    if more:
                        pool.wait_ge(s_pv[L], at(4, b, 4))
                        spread_v(L, b + 2, p)

                phase(0, 0, True, False)
                phase(1, 1, True, True)
                with pool.Fori(1, B // 2 - 1) as i:
                    phase(2 * i, 0, True, True)
                    phase(2 * i + 1, 1, True, True)
                phase(B - 2, 0, True, True, more=False)
                phase(B - 1, 1, False, True, more=False)
                tail(B - 1, 1)

        @block.scalar
        def _(act):
            def stage_a(i, first, last):
                for p in range(2):
                    act.wait_ge(s_xtp[0], at(1, 2 * i + p, 1))
                    act.copy(XT[0][p][:, :], bank[p][:, 0:S]).then_inc(s_xt[0], 1)
                for p in range(2):
                    b = 2 * i + p
                    act.wait_ge(s_v[0], at(1, b, 1))
                    act.copy(va_(b), bank[4 + 3 * p][:, 0:S].rearrange("q (t d) -> q t d", t=TPB)).then_inc(s_va[0], 1)
                    if not first:
                        act.wait_ge(s_scr[0][p], 32 * i)
                    for n in range(2):
                        act.wait_ge(s_rot, at(2, b, n + 1))
                        act.activation(QR[p][:, n, 1], QR[p][:, n, 0], ACT.Square,
                                       scale=float(np.sqrt(LAM / QSCALE)) if n == 0 else 1.0).then_inc(s_act, 1)
                    for n in range(2):
                        act.wait_ge(s_act, at(2, b, n + 1))
                        act.copy(PR[p][:, n, 0:2], QR[p][:, n]).then_inc(s_hi, 1)
            pairs(act, stage_a)

            for L in range(2):
                def exp(b, p, s):
                    act.wait_ge(s_t[L], at(16, b, s + 1))
                    if not (isinstance(b, int) and 4 * b + s // 4 - 1 <= 0):
                        act.wait_ge(s_pv[L], at(4, b, s // 4 - 1))
                    n = 384 if L == 0 else 512
                    act.activation(PB[s % RING][:, 0:n], TB_[s % 3][:, 0:n], ACT.Exp).then_inc(s_e[L], 1)

                def evac_o(b, p, c):
                    act.wait_ge(s_pv[L], at(4, b, 2 * c + 2))
                    act.copy(OT[p][c][:, :], VB_[:, 0:S]).then_inc(s_o[L], 1)

                def tail_c(c, p, s):
                    if s == 3:
                        act.wait_ge(s_zp, at(1, c, 1))
                        act.copy(ZT[p][:, :], MISC[1][:, 0:S]).then_inc(s_zt, 1)
                    if s == 7:
                        act.wait_ge(s_xtp[1], at(1, c, 1))
                        act.copy(XT[1][p][:, :], MISC[1][:, 0:S]).then_inc(s_xt[1], 1)
                    if s in (8, 10):
                        k = s // 10
                        act.wait_ge(s_h, at(2, c, k + 1))
                        for j in range(2):
                            ins = act.activation(HR[p][:, 2 * k + j], MISC[k][:, j * S:(j + 1) * S], ACT.Relu,
                                                 bias=b1_col[:, 2 * k + j:2 * k + j + 1])
                        ins.then_inc(s_hr, 1)
                    if s == 14:
                        act.wait_ge(s_xtp[2], at(1, c, 1))
                        act.activation(XT[2][p][:, :], MISC[1][:, 0:S], ACT.Identity, bias=b_col,
                                       scale=g_col).then_inc(s_xt[2], 1)
                    if s == 15:
                        act.wait_ge(s_qk1, at(1, c, 1))
                        act.activation(QR1[p][:, 0], MISC[0][:, 0:S], ACT.Identity, bias=bqs_col, scale=QSCALE)
                        act.activation(QR1[p][:, 1], MISC[0][:, S:2 * S], ACT.Identity, bias=bk_col).then_inc(s_qr1, 1)
                        act.wait_ge(s_qr1, at(1, c, 1))
                        if not (isinstance(c, int) and c < 2):
                            act.wait_ge(s_scr[1][p], at(16, c, -16 * p))
                        act.copy(PR1[p][:, :, 0], QR1[p][:, :, :]).then_inc(s_hi1, 1)

                def tail_e(c, p, s):
                    if s == 4:
                        act.wait_ge(s_xtp[3], at(1, c, 1))
                        act.copy(XHL[p][:, 0], MISC[1][:, 0:S]).then_inc(s_xt[3], 1)
                    if s in (6, 8, 11):
                        j = (6, 8, 11).index(s)
                        act.wait_ge(s_gu, at(3, c, j + 1))
                        act.activation(TH[j][:, :], MISC[j > 0][:, 0:S], ACT.Tanh, scale=0.5 * SCALE).then_inc(s_th, 1)

                tail = tail_e if L else tail_c

                def phase(b, p, scores, with_tail):
                    for s in range(H):
                        exp(b, p, s)
                        if s == 10:
                            evac_o(b, p, 0)
                        if with_tail:
                            tail(b - 1, 1 - p, s)
                    evac_o(b, p, 1)
                if L == 0:
                    act.wait_ge(s_prep, 2)
                phases(act, phase)
                for s in range(H):
                    tail(B - 1, 1, s)

        @block.vector
        def _(dve):
            dve.memset(QS[0][0][:, :, :].bitcast(U32), 0).then_inc(s_init[0][0], 1)
            dve.memset(KS[0][0][0:MROW].bitcast(U32), 0).then_inc(s_init[0][0], 1)
            dve.memset(KS[0][0][MROW:P], 1.0).then_inc(s_init[0][0], 1)
            for p in range(2):
                dve.memset(VP[p][:, :, :], 0.0).then_inc(s_vz, 1)
            dve.wait_ge(s_x, 16)

            def held():
                dve.memset(HOLD[:, :], 0.0)

            def variance(n, b, p, chain):
                for t in range(TPB):
                    dve.bn_stats(STAT[:, n, p, t], xs[:, b * TPB + t]).then_inc(chain, 1)
                dve.wait_ge(chain, at(TPB, b, TPB))
                held()
                for t in range(TPB):
                    ins = dve.bn_aggr(MV[:, n, p, t], STAT[:, n, p, t])
                ins.then_inc(s_var[n], 1)

            def normalise(n, b, p):
                dve.wait_ge(s_rstd[n], at(2, b, 2))
                for t in range(TPB):
                    ins = dve.tensor_scalar(XN[n][p][:, t], xs[:, b * TPB + t], MV[:, n, p, t, 0:1], RS[:, n, p, t:t + 1],
                                            ALU.subtract, ALU.mult)
                ins.then_inc(s_xn[n], 1)

            def stage_a(i, first, last):
                for p in range(2):
                    variance(0, 2 * i + p, p, s_stat[0])
                for p in range(2):
                    normalise(0, 2 * i + p, p)
                for p in range(2):
                    b = 2 * i + p
                    for n in range(2):
                        dve.wait_ge(s_qk, at(2, b, n + 1))
                        dve.tensor_tensor(TQ[p][:, n], bank[2 + n + 3 * p][:, :], TAB[:, n], ALU.mult).then_inc(s_mul, 1)
                    for n in range(2):
                        dve.wait_ge(s_hi, at(2, b, n + 1))
                        dve.tensor_tensor(PR[p][:, n, 2:4], QR[p][:, n], PR[p][:, n, 0:2], ALU.subtract).then_inc(s_lo, 1)
            dve.wait_ge(s_c, 64)
            pairs(dve, stage_a)

            dve.tensor_copy(MSK[:, :, :], MSF[:, :, :]).then_inc(s_msk, 1)
            dve.wait_ge(s_wi, 16)
            dve.tensor_copy(WGU[:, :], WI[:, 0:2 * HIDDEN]).then_inc(s_prep, 1)
            dve.tensor_scalar(bqs_col, bq_col, QSCALE, None, ALU.mult).then_inc(s_prep, 1)
            dve.tensor_scalar(WD[:, :, :], WI[:, 2 * HIDDEN:].rearrange("p (n d) -> p n d", n=NG), SCALE, None,
                              ALU.mult).then_inc(s_prep, 1)
            dve.tensor_scalar(gate_row, gate_row, HADAMARD, None, ALU.mult).then_inc(s_prep, 1)
            dve.wait_ge(s_prep, 4)

            for L in range(2):
                NB = 3 if L == 0 else 2

                def maximum(b, p, s):
                    dve.wait_ge(s_s[L], at(16, b, s + 1))
                    w = 384 if L == 0 else 512
                    dve.tensor_reduce(NM[p][:, s, 0:NB], SB_[s % 2][:, 0:w].rearrange("q (n k) -> q n k", n=NB),
                                      AX.X, ALU.max, negate=True).then_inc(s_mx[L], 1)
                    if L == 0 and s % HC == HC - 1:
                        dve.wait_ge(s_mx[L], at(16, b, s + 1))
                        cs = slice(s + 1 - HC, s + 1)
                        dve.tensor_tensor(NMB[p][:, cs], NM[p][:, cs, 1], NM[p][:, cs, 2], ALU.min).then_inc(s_mb, 1)

                def split_max(b, p, c):
                    dve.wait_ge(s_mt[L], at(2, b, c + 1))
                    dve.tensor_copy(MT[p][c][:, 0], MISC[c ^ 1][0:HC, 0:S]).then_inc(s_dve, 1)
                    dve.wait_ge(s_dve, at(2, b, c + 1) + 2 * B * L)
                    dve.tensor_tensor(MT[p][c][:, 1], MISC[c ^ 1][0:HC, 0:S], MT[p][c][:, 0], ALU.subtract).then_inc(s_ms[L], 1)

                def norm_o(c, p):
                    o = MISC[0][:, :].rearrange("q (n r) -> q n r", r=32)
                    dve.wait_ge(s_ot[L], at(1, c, 1))
                    dve.reciprocal(REC[p][:, :, :], o[:, :, 16:18]).then_inc(s_rec[L], 1)
                    dve.wait_ge(s_rec[L], at(1, c, 1))
                    dve.tensor_tensor(Y[p][:, :].rearrange("q (n e d) -> q n e d", e=2, d=HD),
                                      o[:, :, 0:16].rearrange("q n (e d) -> q n e d", e=2),
                                      REC[p][:, :, :].rearrange("q n (e o) -> q n e o", o=1).to_broadcast([P, 16, 2, HD]),
                                      ALU.mult).then_inc(s_y[L], 1)

                def add_stream(c, other, n, done, chain):
                    dve.tensor_tensor(xt_(c), xt_(c), other, ALU.add).then_inc(done, 1)
                    dve.wait_ge(done, at(1, c, 1))
                    held()

                def tail_c(c, p, s):
                    m0 = MISC[0][:, 0:S].rearrange("q (t d) -> q t d", t=TPB)
                    if s == 0:
                        norm_o(c, p)
                    if s == 2:
                        dve.wait_ge(s_z, at(2, c, 1))
                        dve.scalar_tensor_tensor(out=Z[p][:, :], in0=ZG[p][:, :], scalar=1.0, in1=Y[p][:, :],
                                                 op0=ALU.add, op1=ALU.mult).then_inc(s_z, 1)
                    if s == 5:
                        dve.wait_ge(s_wo, at(1, c, 1))
                        add_stream(c, m0, 1, s_res[0], None)
                        variance(1, c, p, s_stat[1])
                    if s == 6:
                        normalise(1, c, p)
                    if s == 12:
                        dve.wait_ge(s_f, at(1, c, 1))
                        dve.wait_ge(s_xb, at(1, c, 1))
                        add_stream(c, m0, 2, s_res[1], None)
                        variance(2, c, p, s_stat[2])
                    if s == 13:
                        normalise(2, c, p)
                    if s == 15:
                        dve.wait_ge(s_v[1], at(1, c, 1))
                        bv = bv_row.rearrange("q (o d) -> q o d", o=1).to_broadcast([P, TPB, D])
                        dve.tensor_tensor(va_(c), MISC[1][:, 0:S].rearrange("q (t d) -> q t d", t=TPB), bv,
                                          ALU.add).then_inc(s_va[1], 1)

                def tail_e(c, p, s):
                    if s == 0:
                        norm_o(c, p)
                        dve.wait_ge(s_y[1], at(1, c, 1))
                        add_stream(c, Y[p][:, :].rearrange("q (t d) -> q t d", t=TPB), 3, s_res[2], None)
                        variance(3, c, p, s_stat[3])
                    if s == 2:
                        normalise(3, c, p)
                    if s == 4:
                        dve.wait_ge(s_xt[3], at(1, c, 1))
                        dve.tensor_tensor(XHL[p][:, 1], MISC[1][:, 0:S], XHL[p][:, 0], ALU.subtract).then_inc(s_xlo, 1)
                    if s in (6, 8, 11):
                        j = (6, 8, 11).index(s)
                        gu = MISC[j > 0]
                        dve.wait_ge(s_th, at(3, c, j + 1))
                        dve.scalar_tensor_tensor(out=GA[j][:, :], in0=TH[j][:, :], scalar=1.0, in1=gu[:, 0:S],
                                                 op0=ALU.add, op1=ALU.mult).then_inc(s_ga, 1)
                        dve.wait_ge(s_ga, at(3, c, j + 1))
                        dve.scalar_tensor_tensor(out=HG[p][:, j], in0=GA[j][:, :], scalar=0.5 * SCALE * SCALE,
                                                 in1=gu[:, S:2 * S], op0=ALU.mult, op1=ALU.mult).then_inc(s_hg, 1)
                    if s == 13:
                        dve.wait_ge(s_dn, at(1, c, 1))
                        dve.tensor_tensor(xt_(c), xt_(c), MISC[0][:, 0:S].rearrange("q (t d) -> q t d", t=TPB),
                                          ALU.add).then_inc(s_xo, 1)

                tail = tail_e if L else tail_c

                for s in range(H):
                    maximum(0, 0, s)
                for c in range(2):
                    split_max(0, 0, c)

                def phase(b, p, scores, with_tail):
                    for s in range(H):
                        if scores:
                            maximum(b + 1, 1 - p, s)
                            if s == 10:
                                split_max(b + 1, 1 - p, 0)
                        if with_tail:
                            tail(b - 1, 1 - p, s)
                    if scores:
                        split_max(b + 1, 1 - p, 1)
                phases(dve, phase)
                for s in range(H):
                    tail(B - 1, 1, s)

        @block.tensor
        def _(pe):
            def norm_t(n, b, p, dst):
                pe.wait_ge(s_xn[n], at(1, b, 1))
                for t in range(TPB):
                    ins = pe.transpose(dst[:, t * P:(t + 1) * P], XN[n][p][:, t], IDF[:, :])
                ins.then_inc(s_xtp[n], 1)

            def stage_a(i, first, last):
                for p in range(2):
                    norm_t(0, 2 * i + p, p, bank[p])
                for p in range(2):
                    b = 2 * i + p
                    xt = XT[0][p]
                    pe.wait_ge(s_xt[0], at(1, b, 1))
                    if not first:
                        pe.wait_ge(s_mul, at(2, b, -2))
                        pe.wait_ge(s_va[0], at(1, b, -1))
                    for n, (w, wr) in enumerate(((wq, wrq), (wk, wrk))):
                        pe.matmul(bank[2 + n + 3 * p][:, 0:S], w, xt[:, :], start=True, stop=True)
                        pe.matmul(bank[2 + n + 3 * p][:, S:2 * S], wr, xt[:, :], start=True, stop=True).then_inc(s_qk, 1)
                    for t in range(TPB):
                        ins = pe.matmul(bank[4 + 3 * p][:, t * D:(t + 1) * D], xt[:, t * P:(t + 1) * P], wv,
                                        start=True, stop=True)
                    ins.then_inc(s_v[0], 1)
            pe.wait_ge(s_w, 16)
            pe.wait_ge(s_c, 64)
            pairs(pe, stage_a)

            pe.wait_ge(s_mul, 2 * B)
            pe.wait_ge(s_va[0], B)
            pe.wait_ge(s_msk, 1)

            for L in range(2):
                def scores(b, p, s):
                    if s % HC == 0:
                        pe.wait_ge(s_st[L][s // HC], at(64, b, 64))
                    if not (isinstance(b, int) and 16 * b + s < 2):
                        pe.wait_ge(s_mx[L], at(16, b, s - 1))
                    q, k, o = QS[L][p][0:MROW, s], KS[L][p][0:MROW, s], SB_[s % 2]
                    if L == 0:
                        pe.matmul(o[:, 0:P], MSK[:, 0], MSK[:, 1], start=True, stop=True)
                        pe.matmul(o[:, 0:P], q[:, 0:P], k[:, 0:P], start=False, stop=True, skip_group_check=True)
                        pe.matmul(o[:, 2 * P:3 * P], MSK[:, 0], MSK[:, 1], start=True, stop=True, skip_group_check=True)
                        ins = pe.matmul(o[:, P:3 * P], q[:, P:2 * P], k[:, :], start=False, stop=True,
                                        skip_group_check=True)
                    else:
                        pe.matmul(o[:, 0:S], q[:, 0:P], k[:, :], start=True, stop=True)
                        ins = pe.matmul(o[:, S:2 * S], q[:, P:2 * P], k[:, :], start=True, stop=True)
                    ins.then_inc(s_s[L], 1)

                def max_rows(b, p, c):
                    if L == 0:
                        pe.wait_ge(s_mb, at(2, b, c + 1))
                    else:
                        pe.wait_ge(s_mx[L], at(16, b, HC * (c + 1)))
                    cs = slice(HC * c, HC * (c + 1))
                    m = MISC[c ^ 1]
                    pe.transpose(m[0:HC, 0:P], NM[p][:, cs, 0], IDF[:, :])
                    pe.transpose(m[0:HC, P:2 * P], NMB[p][:, cs] if L == 0 else NM[p][:, cs, 1],
                                 IDF[:, :]).then_inc(s_mt[L], 1)

                def shifted(b, p, s):
                    if s % HC == 0:
                        pe.wait_ge(s_mi[L][s // HC], at(32, b, 32))
                    first = isinstance(b, int) and b == 0
                    if s >= 3 or not first:
                        pe.wait_ge(s_e[L], at(16, b, s - 2 if s >= 3 else (0, -2, -1)[s]))
                    q, k, o = QS[L][p][:, s], KS[L][p][:, s], TB_[s % 3]
                    if L == 0:
                        pe.matmul(o[:, 0:P], MSK[:, 0], MSK[:, 2], start=True, stop=True)
                        pe.matmul(o[:, 0:S], k[:, 0:P], q[:, :], start=False, stop=True, skip_group_check=True)
                        pe.matmul(o[:, S:S + P], MSK[:, 0], MSK[:, 2], start=True, stop=True, skip_group_check=True)
                        ins = pe.matmul(o[:, S:S + P], k[:, P:2 * P], q[:, P:2 * P], start=False, stop=True,
                                        skip_group_check=True)
                    else:
                        pe.matmul(o[:, 0:S], k[:, 0:P], q[:, :], start=True, stop=True)
                        ins = pe.matmul(o[:, S:2 * S], k[:, P:2 * P], q[:, :], start=True, stop=True)
                    ins.then_inc(s_t[L], 1)

                def pv(b, p, g):
                    pe.wait_ge(s_e[L], at(16, b, 4 * g + 4))
                    if g == 0:
                        pe.wait_ge(s_vp[L], at(1, b, 1))
                    if g % 2 == 0 and not (isinstance(b, int) and 2 * b + g // 2 == 0):
                        pe.wait_ge(s_o[L], at(2, b, g // 2))
                    for kt in range(TPB):
                        for j in range(4):
                            s = 4 * g + j
                            v = VP[p][:, kt, 32 * (8 * (g // 2) + 2 * j + g % 2):][:, 0:32]
                            pr = PB[s % RING]
                            if L == 0 and kt == 1:
                                o, pr = VB_[32 * j:32 * j + 32, P:S], pr[:, S:S + P]
                            else:
                                o, pr = VB_[32 * j:32 * j + 32, 0:S], pr[:, kt * S:(kt + 1) * S]
                            ins = pe.matmul(o, v, pr, start=(g % 2 == 0 and kt == 0), stop=True,
                                            skip_group_check=True)
                    ins.then_inc(s_pv[L], 1)

                def turn_o(c, p, last):
                    pe.wait_ge(s_o[L], at(2, c, 2))
                    if last:
                        pe.wait_ge(s_qr1 if L == 0 else s_xo, at(1, c, 0))
                    else:
                        pe.wait_ge(s_ms[L], at(2, c, 4))
                    for t in range(TPB):
                        for k in range(2):
                            ins = pe.transpose(MISC[0][:, (2 * t + k) * P:(2 * t + k + 1) * P],
                                               OT[p][k][:, t * P:(t + 1) * P], IDF[:, :])
                    ins.then_inc(s_ot[L], 1)

                def tail_c(c, p, s, last, with_scores):
                    if s == 0:
                        turn_o(c, p, last)
                    if s == 3:
                        pe.wait_ge(s_z, at(2, c, 2))
                        if not (isinstance(c, int) and c == 0):
                            pe.wait_ge(s_va[1], at(1, c, 0))
                        for t in range(TPB):
                            ins = pe.transpose(MISC[1][:, t * P:(t + 1) * P], Z[p][:, t * D:(t + 1) * D], IDF[:, :])
                        ins.then_inc(s_zp, 1)
                    if s == 5:
                        pe.wait_ge(s_zt, at(1, c, 1))
                        pe.wait_ge(s_y[0], at(1, c, 1))
                        for t in range(TPB):
                            ins = pe.matmul(MISC[0][:, t * D:(t + 1) * D], ZT[p][:, t * P:(t + 1) * P], wo,
                                            start=True, stop=True)
                        ins.then_inc(s_wo, 1)
                    if s == 7:
                        norm_t(1, c, p, MISC[1])
                    if s in (8, 10):
                        k = s // 10
                        if k == 0:
                            pe.wait_ge(s_xt[1], at(1, c, 1))
                            pe.wait_ge(s_var[1], at(1, c, 1))
                        elif with_scores:
                            pe.wait_ge(s_ms[L], at(2, c, 5))
                        for j in range(2):
                            n = 2 * k + j
                            ins = pe.matmul(MISC[k][:, j * S:(j + 1) * S], wi1[:, n * P:(n + 1) * P], XT[1][p][:, :],
                                            start=True, stop=True)
                        ins.then_inc(s_h, 1)
                    if s == 12:
                        pe.wait_ge(s_hr, at(2, c, 2))
                        for t in range(TPB):
                            for n in range(NI):
                                ins = pe.matmul(MISC[0][:, t * D:(t + 1) * D], HR[p][:, n, t * P:(t + 1) * P], wi2[:, n],
                                                start=(n == 0), stop=(n == NI - 1))
                        ins.then_inc(s_f, 1)
                    if s == 14:
                        norm_t(2, c, p, MISC[1])
                    if s == 15:
                        pe.wait_ge(s_xt[2], at(1, c, 1))
                        pe.wait_ge(s_var[2], at(1, c, 1))
                        for n in range(2):
                            ins = pe.matmul(MISC[0][:, n * S:(n + 1) * S], W1[:, n * D:(n + 1) * D], XT[2][p][:, :],
                                            start=True, stop=True)
                        ins.then_inc(s_qk1, 1)
                        for t in range(TPB):
                            ins = pe.matmul(MISC[1][:, t * D:(t + 1) * D], XT[2][p][:, t * P:(t + 1) * P], W1[:, 2 * D:3 * D],
                                            start=True, stop=True)
                        ins.then_inc(s_v[1], 1)

                def tail_e(c, p, s, last, with_scores):
                    if s == 0:
                        turn_o(c, p, last)
                    if s == 4:
                        if not (isinstance(c, int) and c == 0):
                            pe.wait_ge(s_hg, at(3, c, 0))
                        norm_t(3, c, p, MISC[1])
                    if s in (6, 8, 11):
                        j = (6, 8, 11).index(s)
                        if j == 0:
                            pe.wait_ge(s_y[1], at(1, c, 1))
                            pe.wait_ge(s_xlo, at(1, c, 1))
                        else:
                            pe.wait_ge(s_hg, at(3, c, j))
                            if j == 2 and with_scores:
                                pe.wait_ge(s_ms[L], at(2, c, 5))
                        for n in range(2):
                            w = WGU[:, n * HIDDEN + j * P:n * HIDDEN + (j + 1) * P]
                            for k in range(2):
                                ins = pe.matmul(MISC[j > 0][:, n * S:(n + 1) * S], w, XHL[p][:, k], start=(k == 0),
                                                stop=(k == 1))
                        ins.then_inc(s_gu, 1)
                    if s == 13:
                        pe.wait_ge(s_hg, at(3, c, 3))
                        for t in range(TPB):
                            for n in range(NG):
                                ins = pe.matmul(MISC[0][:, t * D:(t + 1) * D], HG[p][:, n, t * P:(t + 1) * P], WD[:, n],
                                                start=(n == 0), stop=(n == NG - 1))
                        ins.then_inc(s_dn, 1)

                tail = tail_e if L else tail_c

                def phase(b, p, with_scores, with_tail):
                    for s in range(H):
                        if with_scores:
                            scores(b + 1, 1 - p, s)
                        shifted(b, p, s)
                        if s in (5, 9, 13):
                            pv(b, p, s // 4 - 1)
                        if with_scores and s == 9:
                            if with_tail:
                                pe.wait_ge(s_xt[1] if L == 0 else s_hg, at(1, b, 0) if L == 0 else at(3, b, -1))
                            max_rows(b + 1, 1 - p, 0)
                        if with_tail:
                            tail(b - 1, 1 - p, s, False, with_scores)
                    pv(b, p, 3)
                    if with_scores:
                        if with_tail:
                            pe.wait_ge(s_qr1 if L == 0 else s_xo, at(1, b, 0))
                        max_rows(b + 1, 1 - p, 1)

                if L == 1:
                    pe.wait_ge(s_mx[0], 16 * B)
                    pe.wait_ge(s_e[0], 16 * B)
                    pe.wait_ge(s_o[0], 2 * B)
                    pe.wait_ge(s_qr1, B)
                    pe.wait_ge(s_va[1], B)
                    pe.wait_ge(s_wi, 16)
                    pe.wait_ge(s_prep, 4)
                for s in range(H):
                    scores(0, 0, s)
                for c in range(2):
                    max_rows(0, 0, c)
                if L == 0:
                    pe.wait_ge(s_w1, 16)
                phases(pe, phase)
                for s in range(H):
                    tail(B - 1, 1, s, True, False)


def _program_inputs(inputs):
    a = {k: np.asarray(v) for k, v in inputs.items()}
    heads = np.array([head_of_slot(s) for s in range(H)])
    feat = (np.arange(HD)[:, None] + HD * heads[None, :]).reshape(-1)
    rot = ((np.arange(HD)[:, None] + HD // 2) % HD + HD * heads[None, :]).reshape(-1)
    half = HD // 2
    inv = (1.0 / 10000.0 ** (np.arange(half, dtype=np.float32) / np.float32(half))).astype(np.float32)
    ang = np.arange(S, dtype=np.float32)[:, None] * inv[None, :]
    j = np.arange(P) // H
    cos = np.cos(ang).astype(np.float32).T[j % half]
    sin = np.sin(ang).astype(np.float32).T[j % half] * np.where(j < half, -1, 1).astype(np.float32)[:, None]
    qs = np.float32(QSCALE)
    tab = np.stack([np.concatenate([cos * qs, sin * qs], 1), np.concatenate([cos, sin], 1)], 1)
    c = np.ascontiguousarray
    w0 = np.concatenate([a["L0_attn_Wq"][feat].T, a["L0_attn_Wq"][rot].T, a["L0_attn_Wk"][feat].T,
                         a["L0_attn_Wk"][rot].T, a["L0_attn_Wv"].T, a["L0_attn_Wo"].T, a["L0_ffn_W1"],
                         a["L0_ffn_W2"].reshape(NI, P, D).transpose(1, 0, 2).reshape(P, NI * D)], 1)

    def rows(v):
        return np.broadcast_to(v[None, :], (P, D))

    def col(v):
        return v.reshape(-1, P).T

    small = np.concatenate([rows(np.tile(a["L0_attn_gate_w"], H)), rows(a["L0_ffn_b2"]), rows(a["L1_attn_bv"]),
                            rows(a["L1_attn_bv"]), col(a["L0_ffn_b1"]), col(a["L1_attn_ln_g"]), col(a["L1_attn_ln_b"]),
                            col(a["L1_attn_bq"][feat]), col(a["L1_attn_bk"][feat]), col(a["L1_attn_bk"][feat])], 1)
    w1 = np.concatenate([a["L1_attn_Wq"][:, feat], a["L1_attn_Wk"][:, feat], a["L1_attn_Wv"]], 1)
    wint = np.concatenate([a["L1_ffn_w_gate"].T, a["L1_ffn_w_up"].T,
                           a["L1_ffn_w_down"].T.reshape(NG, P, D).transpose(1, 0, 2).reshape(P, NG * D)], 1)
    upper = np.triu(np.ones((P, P), np.float32), 1) * np.float32(-1e30)
    masks = np.stack([np.eye(P, dtype=np.float32), upper, upper.T], 1)
    return {"x": c(a["L0_attn_x"]), "w0": c(w0), "tab": c(tab), "small": c(small), "w1": c(w1), "wint": c(wint),
            "ident": np.eye(P, dtype=np.float32), "masks": c(masks)}


def kernel(**inputs):
    from concourse import bacc
    from concourse.bass_utils import run_bass_kernel_spmd

    nc = bacc.Bacc("TRN2", target_bir_lowering=False, num_devices=1)
    arrays = _program_inputs(inputs)
    args = {n: nc.dram_tensor(f"in_{n}", v.shape, mybir.dt.from_np(v.dtype), kind="ExternalInput").ap()
            for n, v in arrays.items()}
    out = nc.dram_tensor("out_x", (B, S, D), F32, kind="ExternalOutput").ap()
    program(nc, *args.values(), out)
    r = run_bass_kernel_spmd(nc, [{f"in_{n}": v for n, v in arrays.items()}], core_ids=[0])
    return r.results[0]["out_x"]
```

```python
from contextlib import ExitStack

import numpy as np

import concourse.bass as bass
from concourse import mybir

ALU = mybir.AluOpType
ACT = mybir.ActivationFunctionType
AX = mybir.AxisListType
F32 = mybir.dt.float32
F16 = mybir.dt.float16
BF16 = mybir.dt.bfloat16
I32 = mybir.dt.int32
U32 = mybir.dt.uint32

P = 128
B, S, D = 8, 256, 128
H, HD = 16, 8
TPB = S // P
INTER = 512
NI = INTER // P
HIDDEN = 384
NG = HIDDEN // P
HC = H // 2
LAM = 0.1
HADAMARD = 0.05
EPS = 1e-5
SCALE = 1.0 / 127.0
QSCALE = 1.0 / float(np.sqrt(HD))
MROW = 96
RING = 8
GU = (8, 9, 11)


def head_of_slot(s):
    return 2 * (4 * (s // 8) + s % 4) + (s % 8) // 4


def program(nc, x, w0, tab, small, w1, wint, ident, masks, out):
    with ExitStack() as ctx:
        def sb(name, shape, dt=F32):
            return ctx.enter_context(nc.sbuf_tensor(name, shape, dt))

        def sem(name):
            return ctx.enter_context(nc.semaphore(name))

        scr = [nc.dram_tensor("scr0", [B, 2, 4, P, S], F16, kind="Internal").ap(),
               nc.dram_tensor("scr1", [B, 2, 2, P, S], F16, kind="Internal").ap()]
        NS = [4, 2]

        xs = sb("xs", [P, B * TPB, D])
        W0 = sb("W0", [P, 6 * D + INTER + NI * D])
        TAB = sb("TAB", [P, 2, 2 * S])
        SM = sb("SM", [P, 4 * D + NI + 5])
        W1 = sb("W1", [P, 3 * D])
        WI = sb("WI", [P, 3 * HIDDEN], I32)
        IDF = sb("IDF", [P, P])
        MSF = sb("MSF", [P, 3, P])
        MSK = sb("MSK", [P, 3, P], BF16)
        WGU = sb("WGU", [P, 2 * HIDDEN], F16)
        WD = sb("WD", [P, NG, D])
        wq, wrq, wk, wrk, wv, wo = [W0[:, n * D:(n + 1) * D] for n in range(6)]
        wi1 = W0[:, 6 * D:6 * D + INTER]
        wi2 = W0[:, 6 * D + INTER:].rearrange("p (n d) -> p n d", n=NI)
        gate_row, b2_row, bv_row = [SM[:, n * D:(n + 1) * D] for n in range(3)]
        b1_col = SM[:, 4 * D:4 * D + NI]
        g_col, b_col, bq_col, bk_col, bqs_col = [SM[:, 4 * D + NI + n:4 * D + NI + n + 1] for n in range(5)]
        EPSC = sb("EPSC", [P, 2, TPB])
        STAT = sb("STAT", [P, 4, 2, TPB, 6])
        MV = sb("MV", [P, 4, 2, TPB, 2])
        VE = sb("VE", [P, 4, 2, TPB])
        RS = sb("RS", [P, 4, 2, TPB])
        HOLD = sb("HOLD", [P, 1])
        HELD = sb("HELD", [P, H])
        XN = [[sb(f"XN{n}{p}", [P, TPB, D]) for p in range(2)] for n in range(4)]
        XT = [[sb(f"XT{n}{p}", [P, S]) for p in range(2)] for n in range(3)]
        XHL = [sb(f"XHL{p}", [P, 2, S], F16) for p in range(2)]
        TQ = [sb(f"TQ{p}", [P, 2, 2 * S]) for p in range(2)]
        QR = [sb(f"QR{p}", [P, 2, 2, S]) for p in range(2)]
        PR = [sb(f"PR{p}", [P, 2, 4, S], F16) for p in range(2)]
        QR1 = [sb(f"QR1{p}", [P, 2, S]) for p in range(2)]
        PR1 = [sb(f"PR1{p}", [P, 2, 2, S], F16) for p in range(2)]
        VA = sb("VA", [P, B * TPB, D])
        VP = [sb(f"VP{p}", [P, TPB, H * 32]) for p in range(2)]
        QS = [[sb(f"QS{L}{p}", [P, H, S], F16) for p in range(2)] for L in range(2)]
        KS = [[sb(f"KS{L}{p}", [P, H, S], F16) for p in range(2)] for L in range(2)]
        PB = [sb(f"PB{n}", [P, 2 * S]) for n in range(RING)]
        NM = [sb(f"NM{p}", [P, H, 3]) for p in range(2)]
        NMB = [sb(f"NMB{p}", [P, H]) for p in range(2)]
        MT = [[sb(f"MT{p}{c}", [HC, 2, S], F16) for c in range(2)] for p in range(2)]
        OT = [[sb(f"OT{p}{c}", [P, S]) for c in range(2)] for p in range(2)]
        REC = [sb(f"REC{p}", [P, 16, 2]) for p in range(2)]
        Y = [sb(f"Y{p}", [P, TPB * D]) for p in range(2)]
        ZG = [sb(f"ZG{p}", [P, TPB * D]) for p in range(2)]
        Z = [sb(f"Z{p}", [P, TPB * D]) for p in range(2)]
        ZT = [sb(f"ZT{p}", [P, S]) for p in range(2)]
        HR = [TQ[p][:, :, :].rearrange("q a (b t) -> q (a b) t", t=S) for p in range(2)]
        TH = [sb(f"TH{j}", [P, S]) for j in range(NG)]
        GA = [sb(f"GA{j}", [P, S]) for j in range(NG)]
        HG = [QR[p][:, :, :, :].rearrange("q a b t -> q (a b) t")[:, 0:NG] for p in range(2)]

        bank = [ctx.enter_context(nc.psum_tensor(f"bank{n}", [P, 512], F32)) for n in range(8)]
        SB_, TB_, VB_, MISC = bank[0:3], bank[3:5], bank[5], bank[6:8]

        s_x, s_w, s_c, s_w1, s_wi = sem("x_loaded"), sem("w0_loaded"), sem("tables_loaded"), sem("w1_loaded"), sem("wint_loaded")
        s_out = sem("out_stored")
        s_init = [[sem(f"stacks_cleared_{L}{p}") for p in range(2)] for L in range(2)]
        s_vz = sem("v_spread_cleared")
        s_msk = sem("masks_narrowed")
        s_prep = sem("weights_prepared")
        s_pool = sem("pool_chain")
        s_act = sem("act_chain")
        s_var = [sem(f"variance_{n}") for n in range(4)]
        s_stat = [sem(f"half_stats_{n}") for n in range(4)]
        s_res = [sem(f"stream_{n}") for n in range(3)]
        s_rec = [sem(f"o_reciprocals_{L}") for L in range(2)]
        s_rstd = [sem(f"rstd_{n}") for n in range(4)]
        s_xn = [sem(f"normed_{n}") for n in range(4)]
        s_xtp = [sem(f"normedT_psum_{n}") for n in range(4)]
        s_xt = [sem(f"normedT_{n}") for n in range(4)]
        s_xlo = sem("normedT_lo")
        s_qk = sem("rope_qk_psum")
        s_v = [sem("v_psum_0"), sem("v_psum_1")]
        s_va = [sem("v_stored_0"), sem("v_stored_1")]
        s_mul = sem("rope_products")
        s_rot = sem("rope_sums")
        s_hi = sem("hi_0")
        s_lo = [sem("lo_q"), sem("lo_k")]
        s_scr = [[sem(f"scratch_{L}{p}") for p in range(2)] for L in range(2)]
        s_qk1 = sem("qk1_psum")
        s_qr1 = sem("qk1_biased")
        s_hi1, s_lo1 = sem("hi_1"), sem("lo_1")
        s_st = [[sem(f"stack_{L}{c}") for c in range(2)] for L in range(2)]
        s_s = [sem(f"scores_{L}") for L in range(2)]
        s_mx = [sem(f"maxima_{L}") for L in range(2)]
        s_mb = sem("maxima_merged")
        s_mt = [sem(f"maxima_rows_psum_{L}") for L in range(2)]
        s_mh = [sem(f"maxima_hi_{L}") for L in range(2)]
        s_ms = [sem(f"maxima_rows_{L}") for L in range(2)]
        s_mi = [[sem(f"maxima_in_{L}{c}") for c in range(2)] for L in range(2)]
        s_t = [sem(f"shifted_scores_{L}") for L in range(2)]
        s_e = [sem(f"probs_{L}") for L in range(2)]
        s_cut = sem("probs_masked")
        s_pv = [sem(f"pv_groups_{L}") for L in range(2)]
        s_vp = [sem(f"v_spread_{L}") for L in range(2)]
        s_o = [sem(f"o_evacuated_{L}") for L in range(2)]
        s_ot = [sem(f"o_tokens_psum_{L}") for L in range(2)]
        s_y = [sem(f"o_normalised_{L}") for L in range(2)]
        s_z = sem("gated")
        s_zp, s_zt = sem("gatedT_psum"), sem("gatedT")
        s_wo = sem("wo_psum")
        s_xb = sem("x_plus_b2")
        s_h, s_hr = sem("ffn0_hidden_psum"), sem("ffn0_hidden")
        s_f = sem("ffn0_psum")
        s_gu, s_th, s_ga, s_hg = sem("gate_up_psum"), sem("tanh"), sem("gate_part"), sem("ffn1_hidden")
        s_dn = sem("ffn1_psum")
        s_xo = sem("x_final")

        block = ctx.enter_context(nc.Block())

        def at(per, b, k):
            return b * per + k

        def xt_(b):
            return xs[:, bass.ds(b * TPB, TPB), :]

        def va_(b):
            return VA[:, bass.ds(b * TPB, TPB), :]

        def pairs(eng, body):
            body(0, True, False)
            with eng.Fori(1, B // 2 - 1) as i:
                body(i, False, False)
            body(B // 2 - 1, False, True)

        def phases(eng, phase):
            def body(i, first, last):
                phase(2 * i, 0, True, not first)
                phase(2 * i + 1, 1, not last, True)
            pairs(eng, body)

        @block.sync
        def _(sp):
            sp.dma_start(xs[:, :, :], x.rearrange("b (t p) d -> p (b t) d", p=P)).then_inc(s_x, 16)
            sp.dma_start(W0[:, :], w0).then_inc(s_w, 16)
            sp.dma_start(IDF[:, :], ident).then_inc(s_c, 16)
            sp.dma_start(TAB[:, :, :], tab).then_inc(s_c, 16)
            sp.dma_start(MSF[:, :, :], masks).then_inc(s_c, 16)
            sp.dma_start(SM[:, :], small).then_inc(s_c, 16)
            sp.dma_start(W1[:, :], w1).then_inc(s_w1, 16)
            sp.dma_start(WI[:, :], wint).then_inc(s_wi, 16)

            def load_stack(L, b, p, c):
                R = NS[L] * HD
                h = R // 2
                cs = slice(HC * c, HC * (c + 1))
                sq, sk = [scr[L][bass.ds(b, 1), n].rearrange("o s (d h) t -> (o s d) h t", h=H) for n in range(2)]
                for dst, src in ((QS[L][p][0:R, cs], sq[:, cs]), (QS[L][p][R:R + h, cs], sq[0:h, cs]),
                                 (KS[L][p][0:h, cs], sk[0:h, cs]), (KS[L][p][h:h + R, cs], sk[:, cs])):
                    sp.dma_start(dst, src).then_inc(s_st[L][c], 16)

            def first_stacks(L, stored):
                for b in range(2):
                    sp.wait_ge(s_init[L][b], 3)
                    sp.wait_ge(s_scr[L][b], stored[b])
                    for c in range(2):
                        if b == 1:
                            sp.wait_ge(s_st[L][c], 64)
                        load_stack(L, b, b, c)

            def store_parts(i, first, last):
                for p in range(2):
                    b = 2 * i + p
                    for n in range(2):
                        sp.wait_ge(s_lo[n], at(1, b, 1))
                        sp.dma_start(scr[0][bass.ds(b, 1), n].rearrange("o s f t -> f (o s) t"),
                                     PR[p][:, n]).then_inc(s_scr[0][p], 16)
                if first:
                    first_stacks(0, (32, 32))
            pairs(sp, store_parts)

            def load_max(L, b, p, c):
                sp.wait_ge(s_ms[L], at(2, b, c + 1))
                for n in range(2):
                    sp.dma_start(QS[L][p][MROW + n:MROW + n + 1, HC * c:HC * (c + 1), :],
                                 MT[p][c][:, n, :]).then_inc(s_mi[L][c], 16)

            def store1(b, p):
                sp.wait_ge(s_lo1, at(1, b, 1))
                for n in range(2):
                    sp.dma_start(scr[1][bass.ds(b, 1), n].rearrange("o s f t -> f (o s) t"),
                                 PR1[p][:, n]).then_inc(s_scr[1][p], 16)

            def store_out(b, p):
                sp.wait_ge(s_xo, at(1, b, 1))
                sp.dma_start(out[bass.ds(b, 1)].rearrange("o (t p) d -> p (o t) d", p=P), xt_(b)).then_inc(s_out, 16)

            for L in range(2):
                def phase(b, p, scores, tail, more=True):
                    load_max(L, b, p, 1)
                    if more:
                        sp.wait_ge(s_t[L], at(16, b, HC))
                        load_stack(L, b + 2, p, 0)
                    if scores:
                        load_max(L, b + 1, 1 - p, 0)
                    if tail:
                        (store1 if L == 0 else store_out)(b - 1, 1 - p)
                    if more:
                        sp.wait_ge(s_t[L], at(16, b, H))
                        load_stack(L, b + 2, p, 1)

                if L == 0:
                    load_max(0, 0, 0, 0)
                phase(0, 0, True, False)
                phase(1, 1, True, True)
                with sp.Fori(1, B // 2 - 1) as i:
                    phase(2 * i, 0, True, True)
                    phase(2 * i + 1, 1, True, True)
                if L == 0:
                    first_stacks(1, (96, 64))
                phase(B - 2, 0, True, True, more=False)
                phase(B - 1, 1, False, True, more=False)
                if L == 0:
                    load_max(1, 0, 0, 0)
                (store1 if L == 0 else store_out)(B - 1, 1)
                if L == 0:
                    for p in range(2):
                        sp.wait_ge(s_scr[1][p], 16 * B)
            sp.wait_ge(s_out, 16 * B)

        @block.gpsimd
        def _(pool):
            pool.memset(EPSC[:, 0], EPS).then_inc(s_pool, 1)
            pool.memset(EPSC[:, 1], -0.5).then_inc(s_pool, 1)

            def clear_stack(L, p):
                pool.memset(QS[L][p][:, :, :].bitcast(U32), 0).then_inc(s_init[L][p], 1)
                pool.wait_ge(s_init[L][p], 1)
                pool.memset(KS[L][p][0:MROW].bitcast(U32), 0).then_inc(s_init[L][p], 1)
                pool.wait_ge(s_init[L][p], 2)
                pool.memset(KS[L][p][MROW:P], 1.0).then_inc(s_init[L][p], 1)
                pool.wait_ge(s_init[L][p], 3)
            pool.wait_ge(s_pool, 2)
            clear_stack(0, 1)
            pool.wait_ge(s_vz, 2)
            for p in range(2):
                for e in range(2):
                    ones = VP[p][:, :, :].rearrange("q t (c f r) -> q (t c) f r", f=2, r=32)[:, :, e, 16 + e:17 + e]
                    pool.memset(ones, 1.0).then_inc(s_pool, 1)
            pool.wait_ge(s_pool, 6)

            def rstd(n, b, p):
                chain = s_rstd[n]
                pool.wait_ge(s_var[n], at(1, b, 1))
                pool.tensor_tensor(VE[:, n, p], MV[:, n, p, :, 1], EPSC[:, 0], ALU.add).then_inc(chain, 1)
                pool.wait_ge(chain, at(2, b, 1))
                pool.tensor_tensor(RS[:, n, p], VE[:, n, p], EPSC[:, 1], ALU.pow).then_inc(chain, 1)

            def rotate(b, p, first):
                if not first:
                    pool.wait_ge(s_lo[1], at(1, b, -1))
                for n in range(2):
                    pool.wait_ge(s_mul, at(2, b, n + 1))
                    pool.tensor_tensor(QR[p][:, n, 0], TQ[p][:, n, 0:S], TQ[p][:, n, S:2 * S],
                                       ALU.add).then_inc(s_rot, 1)

            def lo_k(b, p):
                pool.wait_ge(s_hi, at(2, b, 2))
                pool.tensor_tensor(PR[p][:, 1, 2:4], QR[p][:, 1], PR[p][:, 1, 0:2], ALU.subtract).then_inc(s_lo[1], 1)

            def stage_a(i, first, last):
                b = 2 * i
                rotate(b, 0, first)
                if not last:
                    rstd(0, b + 2, 0)
                rotate(b + 1, 1, first)
                lo_k(b, 0)
                if not last:
                    rstd(0, b + 3, 1)
                lo_k(b + 1, 1)
            for p in range(2):
                rstd(0, p, p)
            pairs(pool, stage_a)
            clear_stack(1, 0)
            clear_stack(1, 1)

            def spread_v(L, b, p):
                pool.wait_ge(s_va[L], at(1, b, 1))
                dst = VP[p][:, :, :].rearrange("q t (c r) -> q t c r", r=64)
                for e in range(2):
                    ins = pool.tensor_copy(dst[:, :, :, 40 * e:40 * e + 8],
                                           va_(b).rearrange("q t (c f d) -> q t c f d", f=2, d=HD)[:, :, :, e])
                ins.then_inc(s_vp[L], 1)

            def cut(b, p, s):
                pool.wait_ge(s_e[0], at(16, b, s + 1))
                pool.tensor_tensor(HELD[:, s:s + 1], EPSC[:, 0, 0:1], EPSC[:, 0, 0:1], ALU.add)
                pr = PB[s % RING][:, :].rearrange("q (n k) -> q n k", n=2)[:, :, 0:P]
                pool.affine_select(out=pr, in_=pr, compare_op=ALU.is_ge, fill=0.0, base=0, pattern=[[0, 2], [1, P]],
                                   channel_multiplier=-1).then_inc(s_cut, 1)

            def tail_c(c, p, s):
                if s == 2:
                    pool.wait_ge(s_y[0], at(1, c, 1))
                    gb = gate_row.rearrange("q (o d) -> q o d", o=1).to_broadcast([P, TPB, D])
                    yv = Y[p][:, :].rearrange("q (t d) -> q t d", t=TPB)
                    pool.tensor_tensor(ZG[p][:, :].rearrange("q (t d) -> q t d", t=TPB), yv, gb, ALU.mult).then_inc(s_z, 1)
                if s == 5:
                    rstd(1, c, p)
                if s == 8:
                    pool.wait_ge(s_xn[1], at(1, c, 1))
                    b2 = b2_row.rearrange("q (o d) -> q o d", o=1).to_broadcast([P, TPB, D])
                    pool.tensor_tensor(xt_(c), xt_(c), b2, ALU.add).then_inc(s_xb, 1)
                if s == 11:
                    rstd(2, c, p)
                if s == 15:
                    pool.wait_ge(s_hi1, at(1, c, 1))
                    pool.tensor_tensor(PR1[p][:, :, 1], QR1[p][:, :, :], PR1[p][:, :, 0], ALU.subtract).then_inc(s_lo1, 1)

            def tail_e(c, p, s):
                if s == 2:
                    rstd(3, c, p)

            for b in range(2):
                spread_v(0, b, b)
            for L in range(2):
                tail = tail_e if L else tail_c

                def phase(b, p, scores, with_tail):
                    for s in range(H):
                        if L == 0:
                            cut(b, p, s)
                        if with_tail and scores and s == 3:
                            pool.wait_ge(s_pv[L], at(4, b, 0))
                            spread_v(L, b + 1, 1 - p)
                        if with_tail:
                            tail(b - 1, 1 - p, s)
                phases(pool, phase)
                for s in range(H):
                    if L == 0 and s == 3:
                        pool.wait_ge(s_pv[0], 4 * B)
                        for b in range(2):
                            spread_v(1, b, b)
                    tail(B - 1, 1, s)

        @block.scalar
        def _(act):
            def copy_xt(b, p):
                act.wait_ge(s_xtp[0], at(1, b, 1))
                act.copy(XT[0][p][:, :], bank[p][:, 0:S]).then_inc(s_xt[0], 1)

            def stage_a(i, first, last):
                for p in range(2):
                    b = 2 * i + p
                    for n in range(2):
                        act.wait_ge(s_rot, at(2, b, n + 1))
                        act.activation(QR[p][:, n, 1], QR[p][:, n, 0], ACT.Square,
                                       scale=float(np.sqrt(LAM / QSCALE)) if n == 0 else 1.0).then_inc(s_act, 1)
                    act.wait_ge(s_v[0], at(1, b, 1))
                    act.copy(va_(b), bank[4 + 3 * p][:, 0:S].rearrange("q (t d) -> q t d", t=TPB)).then_inc(s_va[0], 1)
                    if not first:
                        act.wait_ge(s_scr[0][p], 32 * i)
                    for n in range(2):
                        act.wait_ge(s_act, at(2, b, n + 1))
                        act.copy(PR[p][:, n, 0:2], QR[p][:, n]).then_inc(s_hi, 1)
                for p in range(2):
                    if not last:
                        copy_xt(2 * i + 2 + p, p)
            for p in range(2):
                copy_xt(p, p)
            pairs(act, stage_a)

            def exp(L, b, p, s):
                act.wait_ge(s_t[L], at(16, b, s + 1))
                if not (isinstance(b, int) and 4 * b + s // 4 - 1 <= 0):
                    act.wait_ge(s_pv[L], at(4, b, s // 4 - 1))
                n = 384 if L == 0 else 512
                act.activation(PB[s % RING][:, 0:n], TB_[s % 2][:, 0:n], ACT.Exp).then_inc(s_e[L], 1)

            def evac_o(L, b, p, c):
                act.wait_ge(s_pv[L], at(4, b, 2 * c + 2))
                act.copy(OT[p][c][:, :], VB_[:, 0:S]).then_inc(s_o[L], 1)

            def tail_c(c, p, s):
                if s == 4:
                    act.wait_ge(s_zp, at(1, c, 1))
                    act.copy(ZT[p][:, :], MISC[1][:, 0:S]).then_inc(s_zt, 1)
                if s == 8:
                    act.wait_ge(s_xtp[1], at(1, c, 1))
                    act.copy(XT[1][p][:, :], MISC[1][:, 0:S]).then_inc(s_xt[1], 1)
                if s in (9, 10):
                    k = s - 9
                    act.wait_ge(s_h, at(2, c, k + 1))
                    for j in range(2):
                        ins = act.activation(HR[p][:, 2 * k + j], MISC[k][:, j * S:(j + 1) * S], ACT.Relu,
                                             bias=b1_col[:, 2 * k + j:2 * k + j + 1])
                    ins.then_inc(s_hr, 1)
                if s == 14:
                    act.wait_ge(s_xtp[2], at(1, c, 1))
                    act.activation(XT[2][p][:, :], MISC[1][:, 0:S], ACT.Identity, bias=b_col,
                                   scale=g_col).then_inc(s_xt[2], 1)
                if s == 15:
                    act.wait_ge(s_qk1, at(1, c, 1))
                    act.activation(QR1[p][:, 0], MISC[0][:, 0:S], ACT.Identity, bias=bqs_col, scale=QSCALE)
                    act.activation(QR1[p][:, 1], MISC[0][:, S:2 * S], ACT.Identity, bias=bk_col).then_inc(s_qr1, 1)
                    act.wait_ge(s_qr1, at(1, c, 1))
                    if not (isinstance(c, int) and c < 2):
                        act.wait_ge(s_scr[1][p], at(16, c, -16 * p))
                    act.copy(PR1[p][:, :, 0], QR1[p][:, :, :]).then_inc(s_hi1, 1)

            def tail_e(c, p, s):
                if s == 6:
                    act.wait_ge(s_xtp[3], at(1, c, 1))
                    act.copy(XHL[p][:, 0], MISC[1][:, 0:S]).then_inc(s_xt[3], 1)
                if s in GU:
                    j = GU.index(s)
                    act.wait_ge(s_gu, at(3, c, j + 1))
                    act.activation(TH[j][:, :], MISC[j % 2][:, 0:S], ACT.Tanh, scale=0.5 * SCALE).then_inc(s_th, 1)

            act.wait_ge(s_prep, 2)
            for L in range(2):
                tail = tail_e if L else tail_c
                if L == 1:
                    act.wait_ge(s_pv[0], 4 * B)

                def phase(b, p, scores, with_tail):
                    for s in range(H):
                        exp(L, b, p, s)
                        if s == 1 and with_tail:
                            evac_o(L, b - 1, 1 - p, 1)
                        if s == 10:
                            evac_o(L, b, p, 0)
                        if with_tail:
                            tail(b - 1, 1 - p, s)
                phases(act, phase)
                evac_o(L, B - 1, 1, 1)
                for s in range(H):
                    tail(B - 1, 1, s)

        @block.vector
        def _(dve):
            dve.memset(QS[0][0][:, :, :].bitcast(U32), 0).then_inc(s_init[0][0], 1)
            dve.memset(KS[0][0][0:MROW].bitcast(U32), 0).then_inc(s_init[0][0], 1)
            dve.memset(KS[0][0][MROW:P], 1.0).then_inc(s_init[0][0], 1)
            for p in range(2):
                dve.memset(VP[p][:, :, :], 0.0).then_inc(s_vz, 1)
            dve.wait_ge(s_x, 16)

            def held():
                dve.memset(HOLD[:, :], 0.0)

            def variance(n, b, p, chain):
                for t in range(TPB):
                    dve.bn_stats(STAT[:, n, p, t], xs[:, b * TPB + t]).then_inc(chain, 1)
                dve.wait_ge(chain, at(TPB, b, TPB))
                held()
                for t in range(TPB):
                    ins = dve.bn_aggr(MV[:, n, p, t], STAT[:, n, p, t])
                ins.then_inc(s_var[n], 1)

            def normalise(n, b, p):
                dve.wait_ge(s_rstd[n], at(2, b, 2))
                for t in range(TPB):
                    ins = dve.tensor_scalar(XN[n][p][:, t], xs[:, b * TPB + t], MV[:, n, p, t, 0:1], RS[:, n, p, t:t + 1],
                                            ALU.subtract, ALU.mult)
                ins.then_inc(s_xn[n], 1)

            def products(b, p):
                for n in range(2):
                    dve.wait_ge(s_qk, at(2, b, n + 1))
                    dve.tensor_tensor(TQ[p][:, n], bank[2 + n + 3 * p][:, :], TAB[:, n], ALU.mult).then_inc(s_mul, 1)

            def lo_q(b, p):
                dve.wait_ge(s_hi, at(2, b, 1))
                dve.tensor_tensor(PR[p][:, 0, 2:4], QR[p][:, 0], PR[p][:, 0, 0:2], ALU.subtract).then_inc(s_lo[0], 1)

            def stage_a(i, first, last):
                b = 2 * i
                products(b, 0)
                if not last:
                    variance(0, b + 2, 0, s_stat[0])
                products(b + 1, 1)
                if not last:
                    normalise(0, b + 2, 0)
                    variance(0, b + 3, 1, s_stat[0])
                lo_q(b, 0)
                if not last:
                    normalise(0, b + 3, 1)
                lo_q(b + 1, 1)
            for p in range(2):
                variance(0, p, p, s_stat[0])
            for p in range(2):
                normalise(0, p, p)
            dve.wait_ge(s_c, 64)
            pairs(dve, stage_a)

            dve.tensor_copy(MSK[:, :, :], MSF[:, :, :]).then_inc(s_msk, 1)
            dve.wait_ge(s_wi, 16)
            dve.tensor_copy(WGU[:, :], WI[:, 0:2 * HIDDEN]).then_inc(s_prep, 1)
            dve.tensor_scalar(bqs_col, bq_col, QSCALE, None, ALU.mult).then_inc(s_prep, 1)
            dve.tensor_scalar(WD[:, :, :], WI[:, 2 * HIDDEN:].rearrange("p (n d) -> p n d", n=NG), SCALE, None,
                              ALU.mult).then_inc(s_prep, 1)
            dve.tensor_scalar(gate_row, gate_row, HADAMARD, None, ALU.mult).then_inc(s_prep, 1)
            dve.wait_ge(s_prep, 4)

            def maximum(L, b, p, s):
                n = 3 if L == 0 else 2
                dve.wait_ge(s_s[L], at(16, b, s + 1))
                w = 384 if L == 0 else 512
                dve.tensor_reduce(NM[p][:, s, 0:n], SB_[s % 3][:, 0:w].rearrange("q (n k) -> q n k", n=n),
                                  AX.X, ALU.max, negate=True).then_inc(s_mx[L], 1)
                if L == 0 and s % HC == HC - 1:
                    dve.wait_ge(s_mx[L], at(16, b, s + 1))
                    cs = slice(s + 1 - HC, s + 1)
                    dve.tensor_tensor(NMB[p][:, cs], NM[p][:, cs, 1], NM[p][:, cs, 2], ALU.min).then_inc(s_mb, 1)

            def split_max(L, b, p, c):
                dve.wait_ge(s_mt[L], at(2, b, c + 1))
                dve.tensor_copy(MT[p][c][:, 0], MISC[1][0:HC, 0:S]).then_inc(s_mh[L], 1)
                dve.wait_ge(s_mh[L], at(2, b, c + 1))
                dve.tensor_tensor(MT[p][c][:, 1], MISC[1][0:HC, 0:S], MT[p][c][:, 0], ALU.subtract).then_inc(s_ms[L], 1)

            def norm_o(L, c, p):
                o = MISC[0][:, :].rearrange("q (n r) -> q n r", r=32)
                dve.wait_ge(s_ot[L], at(1, c, 1))
                dve.reciprocal(REC[p][:, :, :], o[:, :, 16:18]).then_inc(s_rec[L], 1)
                dve.wait_ge(s_rec[L], at(1, c, 1))
                dve.tensor_tensor(Y[p][:, :].rearrange("q (n e d) -> q n e d", e=2, d=HD),
                                  o[:, :, 0:16].rearrange("q n (e d) -> q n e d", e=2),
                                  REC[p][:, :, :].rearrange("q n (e o) -> q n e o", o=1).to_broadcast([P, 16, 2, HD]),
                                  ALU.mult).then_inc(s_y[L], 1)

            def add_stream(c, other, done):
                dve.tensor_tensor(xt_(c), xt_(c), other, ALU.add).then_inc(done, 1)
                dve.wait_ge(done, at(1, c, 1))
                held()

            m0 = MISC[0][:, 0:S].rearrange("q (t d) -> q t d", t=TPB)

            def tail_c(c, p, s):
                if s == 2:
                    norm_o(0, c, p)
                if s == 3:
                    dve.wait_ge(s_z, at(2, c, 1))
                    dve.scalar_tensor_tensor(out=Z[p][:, :], in0=ZG[p][:, :], scalar=1.0, in1=Y[p][:, :],
                                             op0=ALU.add, op1=ALU.mult).then_inc(s_z, 1)
                if s == 5:
                    dve.wait_ge(s_wo, at(1, c, 1))
                    add_stream(c, m0, s_res[0])
                    variance(1, c, p, s_stat[1])
                if s == 7:
                    normalise(1, c, p)
                if s == 11:
                    dve.wait_ge(s_f, at(1, c, 1))
                    dve.wait_ge(s_xb, at(1, c, 1))
                    add_stream(c, m0, s_res[1])
                    variance(2, c, p, s_stat[2])
                if s == 13:
                    normalise(2, c, p)
                if s == 15:
                    dve.wait_ge(s_v[1], at(1, c, 1))
                    bv = bv_row.rearrange("q (o d) -> q o d", o=1).to_broadcast([P, TPB, D])
                    dve.tensor_tensor(va_(c), MISC[1][:, 0:S].rearrange("q (t d) -> q t d", t=TPB), bv,
                                      ALU.add).then_inc(s_va[1], 1)

            def tail_e(c, p, s):
                if s == 2:
                    norm_o(1, c, p)
                    dve.wait_ge(s_y[1], at(1, c, 1))
                    add_stream(c, Y[p][:, :].rearrange("q (t d) -> q t d", t=TPB), s_res[2])
                    variance(3, c, p, s_stat[3])
                if s == 4:
                    normalise(3, c, p)
                if s == 6:
                    dve.wait_ge(s_xt[3], at(1, c, 1))
                    dve.tensor_tensor(XHL[p][:, 1], MISC[1][:, 0:S], XHL[p][:, 0], ALU.subtract).then_inc(s_xlo, 1)
                if s in GU:
                    j = GU.index(s)
                    gu = MISC[j % 2]
                    dve.wait_ge(s_th, at(3, c, j + 1))
                    dve.scalar_tensor_tensor(out=GA[j][:, :], in0=TH[j][:, :], scalar=1.0, in1=gu[:, 0:S],
                                             op0=ALU.add, op1=ALU.mult).then_inc(s_ga, 1)
                    dve.wait_ge(s_ga, at(3, c, j + 1))
                    dve.scalar_tensor_tensor(out=HG[p][:, j], in0=GA[j][:, :], scalar=0.5 * SCALE * SCALE,
                                             in1=gu[:, S:2 * S], op0=ALU.mult, op1=ALU.mult).then_inc(s_hg, 1)
                if s == 14:
                    dve.wait_ge(s_dn, at(1, c, 1))
                    dve.tensor_tensor(xt_(c), xt_(c), m0, ALU.add).then_inc(s_xo, 1)

            for s in range(H):
                maximum(0, 0, 0, s)
                if s == 12:
                    split_max(0, 0, 0, 0)
            for L in range(2):
                tail = tail_e if L else tail_c

                def phase(b, p, scores, with_tail):
                    for s in range(H):
                        if scores:
                            maximum(L, b + 1, 1 - p, s)
                        if s == 0:
                            split_max(L, b, p, 1)
                        if scores and s == 12:
                            split_max(L, b + 1, 1 - p, 0)
                        if with_tail:
                            tail(b - 1, 1 - p, s)
                phases(dve, phase)
                for s in range(H):
                    if L == 0:
                        maximum(1, 0, 0, s)
                        if s == 12:
                            split_max(1, 0, 0, 0)
                    tail(B - 1, 1, s)

        @block.tensor
        def _(pe):
            def norm_t(n, b, p, dst):
                pe.wait_ge(s_xn[n], at(1, b, 1))
                for t in range(TPB):
                    ins = pe.transpose(dst[:, t * P:(t + 1) * P], XN[n][p][:, t], IDF[:, :])
                ins.then_inc(s_xtp[n], 1)

            def project(b, p, first):
                xt = XT[0][p]
                pe.wait_ge(s_xt[0], at(1, b, 1))
                if not first:
                    pe.wait_ge(s_mul, at(2, b, -2))
                    pe.wait_ge(s_va[0], at(1, b, -1))
                for n, (w, wr) in enumerate(((wq, wrq), (wk, wrk))):
                    pe.matmul(bank[2 + n + 3 * p][:, 0:S], w, xt[:, :], start=True, stop=True)
                    pe.matmul(bank[2 + n + 3 * p][:, S:2 * S], wr, xt[:, :], start=True, stop=True).then_inc(s_qk, 1)
                for t in range(TPB):
                    ins = pe.matmul(bank[4 + 3 * p][:, t * D:(t + 1) * D], xt[:, t * P:(t + 1) * P], wv,
                                    start=True, stop=True)
                ins.then_inc(s_v[0], 1)

            def stage_a(i, first, last):
                for p in range(2):
                    project(2 * i + p, p, first)
                for p in range(2):
                    if not last:
                        norm_t(0, 2 * i + 2 + p, p, bank[p])
            pe.wait_ge(s_w, 16)
            pe.wait_ge(s_c, 64)
            for p in range(2):
                norm_t(0, p, p, bank[p])
            pairs(pe, stage_a)

            pe.wait_ge(s_mul, 2 * B)
            pe.wait_ge(s_va[0], B)
            pe.wait_ge(s_msk, 1)

            def scores(L, b, p, s):
                if s % HC == 0:
                    pe.wait_ge(s_st[L][s // HC], at(64, b, 64))
                if s >= 3 or not (isinstance(b, int) and b == 0):
                    pe.wait_ge(s_mx[L], at(16, b, s - 2 if s >= 3 else (0, -2, -1)[s]))
                q, k, o = QS[L][p][0:MROW, s], KS[L][p][0:MROW, s], SB_[s % 3]
                if L == 0:
                    pe.matmul(o[:, 0:P], MSK[:, 0], MSK[:, 1], start=True, stop=True)
                    pe.matmul(o[:, 0:P], q[:, 0:P], k[:, 0:P], start=False, stop=True, skip_group_check=True)
                    pe.matmul(o[:, 2 * P:3 * P], MSK[:, 0], MSK[:, 1], start=True, stop=True, skip_group_check=True)
                    ins = pe.matmul(o[:, P:3 * P], q[:, P:2 * P], k[:, :], start=False, stop=True,
                                    skip_group_check=True)
                else:
                    pe.matmul(o[:, 0:S], q[:, 0:P], k[:, :], start=True, stop=True)
                    ins = pe.matmul(o[:, S:2 * S], q[:, P:2 * P], k[:, :], start=True, stop=True)
                ins.then_inc(s_s[L], 1)

            def max_rows(L, b, p, c):
                if L == 0:
                    pe.wait_ge(s_mb, at(2, b, c + 1))
                else:
                    pe.wait_ge(s_mx[L], at(16, b, HC * (c + 1)))
                if c == 1 or not (isinstance(b, int) and b == 0):
                    pe.wait_ge(s_ms[L], at(2, b, c))
                cs = slice(HC * c, HC * (c + 1))
                m = MISC[1]
                pe.transpose(m[0:HC, 0:P], NM[p][:, cs, 0], IDF[:, :])
                pe.transpose(m[0:HC, P:2 * P], NMB[p][:, cs] if L == 0 else NM[p][:, cs, 1],
                             IDF[:, :]).then_inc(s_mt[L], 1)

            def shifted(L, b, p, s):
                if s % HC == 0:
                    pe.wait_ge(s_mi[L][s // HC], at(32, b, 32))
                if s >= 2 or not (isinstance(b, int) and b == 0):
                    pe.wait_ge(s_e[L], at(16, b, s - 1))
                q, k, o = QS[L][p][:, s], KS[L][p][:, s], TB_[s % 2]
                pe.matmul(o[:, 0:S], k[:, 0:P], q[:, :], start=True, stop=True)
                if L == 0:
                    ins = pe.matmul(o[:, S:S + P], k[:, P:2 * P], q[:, P:2 * P], start=True, stop=True)
                else:
                    ins = pe.matmul(o[:, S:2 * S], k[:, P:2 * P], q[:, :], start=True, stop=True)
                ins.then_inc(s_t[L], 1)

            def pv(L, b, p, g):
                pe.wait_ge(s_cut if L == 0 else s_e[1], at(16, b, 4 * g + 4))
                if g == 0:
                    pe.wait_ge(s_vp[L], at(1, b, 1))
                if g % 2 == 0 and not (isinstance(b, int) and 2 * b + g // 2 == 0):
                    pe.wait_ge(s_o[L], at(2, b, g // 2))
                for kt in range(TPB):
                    for j in range(4):
                        s = 4 * g + j
                        v = VP[p][:, kt, 32 * (8 * (g // 2) + 2 * j + g % 2):][:, 0:32]
                        pr = PB[s % RING]
                        if L == 0 and kt == 1:
                            o, pr = VB_[32 * j:32 * j + 32, P:S], pr[:, S:S + P]
                        else:
                            o, pr = VB_[32 * j:32 * j + 32, 0:S], pr[:, kt * S:(kt + 1) * S]
                        ins = pe.matmul(o, v, pr, start=(g % 2 == 0 and kt == 0), stop=True, skip_group_check=True)
                ins.then_inc(s_pv[L], 1)

            def turn_o(L, c, p):
                pe.wait_ge(s_o[L], at(2, c, 2))
                if not (isinstance(c, int) and c == 0):
                    pe.wait_ge(s_qr1 if L == 0 else s_xo, at(1, c, 0))
                for t in range(TPB):
                    for k in range(2):
                        ins = pe.transpose(MISC[0][:, (2 * t + k) * P:(2 * t + k + 1) * P],
                                           OT[p][k][:, t * P:(t + 1) * P], IDF[:, :])
                ins.then_inc(s_ot[L], 1)

            def tail_c(c, p, s, m1, m0):
                if s == 2:
                    turn_o(0, c, p)
                if s == 4:
                    pe.wait_ge(s_z, at(2, c, 2))
                    if m1:
                        pe.wait_ge(s_ms[0], at(2, c, 4))
                    for t in range(TPB):
                        ins = pe.transpose(MISC[1][:, t * P:(t + 1) * P], Z[p][:, t * D:(t + 1) * D], IDF[:, :])
                    ins.then_inc(s_zp, 1)
                if s == 5:
                    pe.wait_ge(s_zt, at(1, c, 1))
                    pe.wait_ge(s_y[0], at(1, c, 1))
                    for t in range(TPB):
                        ins = pe.matmul(MISC[0][:, t * D:(t + 1) * D], ZT[p][:, t * P:(t + 1) * P], wo,
                                        start=True, stop=True)
                    ins.then_inc(s_wo, 1)
                if s == 8:
                    norm_t(1, c, p, MISC[1])
                if s in (9, 10):
                    k = s - 9
                    if k == 0:
                        pe.wait_ge(s_xt[1], at(1, c, 1))
                        pe.wait_ge(s_var[1], at(1, c, 1))
                    for j in range(2):
                        n = 2 * k + j
                        ins = pe.matmul(MISC[k][:, j * S:(j + 1) * S], wi1[:, n * P:(n + 1) * P], XT[1][p][:, :],
                                        start=True, stop=True)
                    ins.then_inc(s_h, 1)
                if s == 11:
                    pe.wait_ge(s_hr, at(2, c, 2))
                    for t in range(TPB):
                        for n in range(NI):
                            ins = pe.matmul(MISC[0][:, t * D:(t + 1) * D], HR[p][:, n, t * P:(t + 1) * P], wi2[:, n],
                                            start=(n == 0), stop=(n == NI - 1))
                    ins.then_inc(s_f, 1)
                if s == 14:
                    if m0 is not None:
                        pe.wait_ge(*m0)
                    norm_t(2, c, p, MISC[1])
                if s == 15:
                    pe.wait_ge(s_xt[2], at(1, c, 1))
                    pe.wait_ge(s_var[2], at(1, c, 1))
                    for n in range(2):
                        ins = pe.matmul(MISC[0][:, n * S:(n + 1) * S], W1[:, n * D:(n + 1) * D], XT[2][p][:, :],
                                        start=True, stop=True)
                    ins.then_inc(s_qk1, 1)
                    for t in range(TPB):
                        ins = pe.matmul(MISC[1][:, t * D:(t + 1) * D], XT[2][p][:, t * P:(t + 1) * P], W1[:, 2 * D:3 * D],
                                        start=True, stop=True)
                    ins.then_inc(s_v[1], 1)

            def tail_e(c, p, s, m1, m0):
                if s == 2:
                    turn_o(1, c, p)
                if s == 6:
                    if m1:
                        pe.wait_ge(s_ms[1], at(2, c, 4))
                    norm_t(3, c, p, MISC[1])
                if s in GU:
                    j = GU.index(s)
                    if j == 0:
                        pe.wait_ge(s_y[1], at(1, c, 1))
                        pe.wait_ge(s_xlo, at(1, c, 1))
                    if j == 2:
                        pe.wait_ge(s_hg, at(3, c, 1))
                    for n in range(2):
                        w = WGU[:, n * HIDDEN + j * P:n * HIDDEN + (j + 1) * P]
                        for k in range(2):
                            ins = pe.matmul(MISC[j % 2][:, n * S:(n + 1) * S], w, XHL[p][:, k], start=(k == 0),
                                            stop=(k == 1))
                    ins.then_inc(s_gu, 1)
                if s == 14:
                    pe.wait_ge(s_hg, at(3, c, 3))
                    for t in range(TPB):
                        for n in range(NG):
                            ins = pe.matmul(MISC[0][:, t * D:(t + 1) * D], HG[p][:, n, t * P:(t + 1) * P], WD[:, n],
                                            start=(n == 0), stop=(n == NG - 1))
                    ins.then_inc(s_dn, 1)

            pe.wait_ge(s_w1, 16)
            for s in range(H):
                scores(0, 0, 0, s)
                if s == 11:
                    max_rows(0, 0, 0, 0)
            for L in range(2):
                tail = tail_e if L else tail_c

                def phase(b, p, with_scores, with_tail):
                    c = b - 1
                    for s in range(H):
                        if with_scores:
                            scores(L, b + 1, 1 - p, s)
                        shifted(L, b, p, s)
                        if s == 0:
                            if L == 0 and not (isinstance(b, int) and b < 2):
                                pe.wait_ge(s_va[1], at(1, c, 0))
                            max_rows(L, b, p, 1)
                        if s == 1 and with_tail:
                            pv(L, c, 1 - p, 3)
                        if s in (5, 9, 13):
                            pv(L, b, p, s // 4 - 1)
                        if with_tail:
                            tail(c, 1 - p, s, True, (s_ms[L], at(2, b, 3)) if with_scores else None)
                        if with_scores and s == 11:
                            if L == 1 and with_tail:
                                pe.wait_ge(s_hg, at(3, c, 2))
                            max_rows(L, b + 1, 1 - p, 0)

                phases(pe, phase)
                if L == 0:
                    pe.wait_ge(s_mx[0], 16 * B)
                    pe.wait_ge(s_prep, 4)
                for s in range(H):
                    if L == 0:
                        scores(1, 0, 0, s)
                    if s == 1:
                        pv(L, B - 1, 1, 3)
                    if L == 0 and s == 4:
                        pe.wait_ge(s_va[1], B - 1)
                    tail(B - 1, 1, s, False, (s_ms[1], 1) if L == 0 else None)
                    if L == 0 and s == 11:
                        max_rows(1, 0, 0, 0)
                if L == 0:
                    pe.wait_ge(s_e[0], 16 * B)
                    pe.wait_ge(s_o[0], 2 * B)
                    pe.wait_ge(s_qr1, B)
                    pe.wait_ge(s_va[1], B)


def _program_inputs(inputs):
    a = {k: np.asarray(v) for k, v in inputs.items()}
    heads = np.array([head_of_slot(s) for s in range(H)])
    feat = (np.arange(HD)[:, None] + HD * heads[None, :]).reshape(-1)
    rot = ((np.arange(HD)[:, None] + HD // 2) % HD + HD * heads[None, :]).reshape(-1)
    half = HD // 2
    inv = (1.0 / 10000.0 ** (np.arange(half, dtype=np.float32) / np.float32(half))).astype(np.float32)
    ang = np.arange(S, dtype=np.float32)[:, None] * inv[None, :]
    j = np.arange(P) // H
    cos = np.cos(ang).astype(np.float32).T[j % half]
    sin = np.sin(ang).astype(np.float32).T[j % half] * np.where(j < half, -1, 1).astype(np.float32)[:, None]
    qs = np.float32(QSCALE)
    tab = np.stack([np.concatenate([cos * qs, sin * qs], 1), np.concatenate([cos, sin], 1)], 1)
    c = np.ascontiguousarray
    w0 = np.concatenate([a["L0_attn_Wq"][feat].T, a["L0_attn_Wq"][rot].T, a["L0_attn_Wk"][feat].T,
                         a["L0_attn_Wk"][rot].T, a["L0_attn_Wv"].T, a["L0_attn_Wo"].T, a["L0_ffn_W1"],
                         a["L0_ffn_W2"].reshape(NI, P, D).transpose(1, 0, 2).reshape(P, NI * D)], 1)

    def rows(v):
        return np.broadcast_to(v[None, :], (P, D))

    def col(v):
        return v.reshape(-1, P).T

    small = np.concatenate([rows(np.tile(a["L0_attn_gate_w"], H)), rows(a["L0_ffn_b2"]), rows(a["L1_attn_bv"]),
                            rows(a["L1_attn_bv"]), col(a["L0_ffn_b1"]), col(a["L1_attn_ln_g"]), col(a["L1_attn_ln_b"]),
                            col(a["L1_attn_bq"][feat]), col(a["L1_attn_bk"][feat]), col(a["L1_attn_bk"][feat])], 1)
    w1 = np.concatenate([a["L1_attn_Wq"][:, feat], a["L1_attn_Wk"][:, feat], a["L1_attn_Wv"]], 1)
    wint = np.concatenate([a["L1_ffn_w_gate"].T, a["L1_ffn_w_up"].T,
                           a["L1_ffn_w_down"].T.reshape(NG, P, D).transpose(1, 0, 2).reshape(P, NG * D)], 1)
    upper = np.triu(np.ones((P, P), np.float32), 1) * np.float32(-1e30)
    masks = np.stack([np.eye(P, dtype=np.float32), upper, upper.T], 1)
    return {"x": c(a["L0_attn_x"]), "w0": c(w0), "tab": c(tab), "small": c(small), "w1": c(w1), "wint": c(wint),
            "ident": np.eye(P, dtype=np.float32), "masks": c(masks)}


def kernel(**inputs):
    from concourse import bacc
    from concourse.bass_utils import run_bass_kernel_spmd

    nc = bacc.Bacc("TRN2", target_bir_lowering=False, num_devices=1)
    arrays = _program_inputs(inputs)
    args = {n: nc.dram_tensor(f"in_{n}", v.shape, mybir.dt.from_np(v.dtype), kind="ExternalInput").ap()
            for n, v in arrays.items()}
    out = nc.dram_tensor("out_x", (B, S, D), F32, kind="ExternalOutput").ap()
    program(nc, *args.values(), out)
    r = run_bass_kernel_spmd(nc, [{f"in_{n}": v for n, v in arrays.items()}], core_ids=[0])
    return r.results[0]["out_x"]
```

```python
from contextlib import ExitStack

import numpy as np

import concourse.bass as bass
from concourse import mybir

ALU = mybir.AluOpType
ACT = mybir.ActivationFunctionType
AX = mybir.AxisListType
F32 = mybir.dt.float32
F16 = mybir.dt.float16
BF16 = mybir.dt.bfloat16
I32 = mybir.dt.int32
U32 = mybir.dt.uint32

P = 128
B, S, D = 8, 256, 128
H, HD = 16, 8
TPB = S // P
INTER = 512
NI = INTER // P
HIDDEN = 384
NG = HIDDEN // P
HC = H // 2
LAM = 0.1
HADAMARD = 0.05
EPS = 1e-5
TWO_ONES = 0x3C003C00
SCALE = 1.0 / 127.0
QSCALE = 1.0 / float(np.sqrt(HD))
MROW = 96
RING = 8
GU = (11, 12, 13)
M0 = (10, 10)
M1 = (1, 0)
PV = ((6, 10, 14), (6, 10, 14))


def head_of_slot(s):
    return 2 * (4 * (s // 8) + s % 4) + (s % 8) // 4


def score_bank(s):
    return 1 if s % H == H - 1 else s % H % 3


def bank_free(s):
    t = s - 1
    while score_bank(t) != score_bank(s):
        t -= 1
    return t + 1


def program(nc, x, w0, tab, small, w1, wint, ident, masks, out):
    with ExitStack() as ctx:
        def sb(name, shape, dt=F32):
            return ctx.enter_context(nc.sbuf_tensor(name, shape, dt))

        def sem(name):
            return ctx.enter_context(nc.semaphore(name))

        scr = [nc.dram_tensor("scr0", [B, 2, 4, P, S], F16, kind="Internal").ap(),
               nc.dram_tensor("scr1", [B, 2, 2, P, S], F16, kind="Internal").ap()]
        NS = [4, 2]

        xs = sb("xs", [P, B * TPB, D])
        W0 = sb("W0", [P, 6 * D + INTER + NI * D])
        TAB = sb("TAB", [P, 2, 2 * S])
        SM = sb("SM", [P, 4 * D + NI + 5])
        W1 = sb("W1", [P, 3 * D])
        WI = sb("WI", [P, 3 * HIDDEN], I32)
        IDF = sb("IDF", [P, P])
        MSF = sb("MSF", [P, 3, P])
        MSK = sb("MSK", [P, 3, P], BF16)
        WGU = sb("WGU", [P, 2 * HIDDEN], F16)
        WD = sb("WD", [P, NG, D])
        wq, wrq, wk, wrk, wv, wo = [W0[:, n * D:(n + 1) * D] for n in range(6)]
        wi1 = W0[:, 6 * D:6 * D + INTER]
        wi2 = W0[:, 6 * D + INTER:].rearrange("p (n d) -> p n d", n=NI)
        gate_row, b2_row, bv_row = [SM[:, n * D:(n + 1) * D] for n in range(3)]
        b1_col = SM[:, 4 * D:4 * D + NI]
        g_col, b_col, bq_col, bk_col, bqs_col = [SM[:, 4 * D + NI + n:4 * D + NI + n + 1] for n in range(5)]
        EPSC = sb("EPSC", [P, 3, TPB])
        NMN = sb("NMN", [P, 2, TPB])
        NRS = sb("NRS", [P, 2, TPB])
        ZO = sb("ZO", [P, 2])
        STAT = sb("STAT", [P, 4, 2, TPB, 6])
        MV = sb("MV", [P, 4, 2, TPB, 2])
        VE = sb("VE", [P, 4, 2, TPB])
        RS = sb("RS", [P, 4, 2, TPB])
        HOLD = sb("HOLD", [P, 1])
        HELD = sb("HELD", [P, H])
        HOLDA = sb("HOLDA", [P, 2])
        XN = [[sb(f"XN{n}{p}", [P, TPB, D]) for p in range(2)] for n in range(4)]
        XT = [[sb(f"XT{n}{p}", [P, S]) for p in range(2)] for n in range(3)]
        XHL = [sb(f"XHL{p}", [P, 2, S], F16) for p in range(2)]
        TQ = [sb(f"TQ{p}", [P, 2, 2 * S]) for p in range(2)]
        QR = [sb(f"QR{p}", [P, 2, 2, S]) for p in range(2)]
        PR = [sb(f"PR{p}", [P, 2, 4, S], F16) for p in range(2)]
        QR1 = [sb(f"QR1{p}", [P, 2, S]) for p in range(2)]
        PR1 = [sb(f"PR1{p}", [P, 2, 2, S], F16) for p in range(2)]
        VA = sb("VA", [P, B * TPB, D])
        VP = [sb(f"VP{p}", [P, TPB, H * 32]) for p in range(2)]
        QS = [[sb(f"QS{L}{p}", [P, H, S], F16) for p in range(2)] for L in range(2)]
        KS = [[sb(f"KS{L}{p}", [P, H, S], F16) for p in range(2)] for L in range(2)]
        PB = [sb(f"PB{n}", [P, 2 * S]) for n in range(RING)]
        NM = [sb(f"NM{p}", [P, H, 3]) for p in range(2)]
        NMB = [sb(f"NMB{p}", [P, H]) for p in range(2)]
        MT = [[sb(f"MT{p}{c}", [HC, 2, S], F16) for c in range(2)] for p in range(2)]
        OT = [[sb(f"OT{p}{c}", [P, S]) for c in range(2)] for p in range(2)]
        REC = [sb(f"REC{p}", [P, 16, 2]) for p in range(2)]
        Y = [sb(f"Y{p}", [P, TPB * D]) for p in range(2)]
        ZG = [sb(f"ZG{p}", [P, TPB * D]) for p in range(2)]
        Z = [sb(f"Z{p}", [P, TPB * D]) for p in range(2)]
        ZT = [sb(f"ZT{p}", [P, S]) for p in range(2)]
        HR = [TQ[p][:, :, :].rearrange("q a (b t) -> q (a b) t", t=S) for p in range(2)]
        TH = [sb(f"TH{j}", [P, S]) for j in range(NG)]
        GS = [sb(f"GS{j}", [P, 2 * S]) for j in range(NG)]
        GA = [sb(f"GA{j}", [P, S]) for j in range(2)]
        HG = [QR[p][:, :, :, :].rearrange("q a b t -> q (a b) t")[:, 0:NG] for p in range(2)]

        bank = [ctx.enter_context(nc.psum_tensor(f"bank{n}", [P, 512], F32)) for n in range(8)]
        SB_, TB_, VB_, MISC = bank[0:3], bank[3:5], bank[5], bank[6:8]

        s_x, s_w, s_c, s_w1, s_wi = sem("x_loaded"), sem("w0_loaded"), sem("constants_loaded"), sem("w1_loaded"), sem("wint_loaded")
        s_xr, s_id, s_tab = sem("rest_of_x_loaded"), sem("identity_loaded"), sem("rope_tables_loaded")
        s_out = sem("out_stored")
        s_init = [[sem(f"stacks_cleared_{L}{p}") for p in range(2)] for L in range(2)]
        s_ones = [sem("stack_ones_0"), sem("stack_ones_1")]
        s_vz = sem("v_spread_cleared")
        s_msk = sem("masks_narrowed")
        s_prep = sem("weights_prepared")
        s_pool = sem("pool_chain")
        s_act = sem("act_chain")
        s_var = [sem(f"variance_{n}") for n in range(4)]
        s_stat = [sem(f"half_stats_{n}") for n in range(4)]
        s_res = [sem(f"stream_{n}") for n in range(3)]
        s_rec = [sem(f"o_reciprocals_{L}") for L in range(2)]
        s_rstd = [sem(f"rstd_{n}") for n in range(4)]
        s_xn = [sem(f"normed_{n}") for n in range(4)]
        s_xtp = [sem(f"normedT_psum_{n}") for n in range(4)]
        s_xt = [sem(f"normedT_{n}") for n in range(4)]
        s_xlo = sem("normedT_lo")
        s_qk = sem("rope_qk_psum")
        s_v = [sem("v_psum_0"), sem("v_psum_1")]
        s_va = [sem("v_stored_0"), sem("v_stored_1")]
        s_mul = sem("rope_products")
        s_rot = sem("rope_sums")
        s_hi = sem("hi_0")
        s_lo = [sem("lo_q"), sem("lo_k"), sem("lo_k_square")]
        s_scr = [[sem(f"scratch_{L}{p}") for p in range(2)] for L in range(2)]
        s_qk1 = sem("qk1_psum")
        s_qr1 = sem("qk1_biased")
        s_hi1, s_lo1 = sem("hi_1"), sem("lo_1")
        s_st = [[sem(f"stack_{L}{c}") for c in range(2)] for L in range(2)]
        s_s = [sem(f"scores_{L}") for L in range(2)]
        s_mx = [sem(f"maxima_{L}") for L in range(2)]
        s_mb = sem("maxima_merged")
        s_mt = [sem(f"maxima_rows_psum_{L}") for L in range(2)]
        s_mh = [sem(f"maxima_hi_{L}") for L in range(2)]
        s_ms = [sem(f"maxima_rows_{L}") for L in range(2)]
        s_mi = [[sem(f"maxima_in_{L}{c}") for c in range(2)] for L in range(2)]
        s_t = [sem(f"shifted_scores_{L}") for L in range(2)]
        s_e = [sem(f"probs_{L}") for L in range(2)]
        s_cut = sem("probs_masked")
        s_pv = [sem(f"pv_groups_{L}") for L in range(2)]
        s_vp = [sem(f"v_spread_{L}") for L in range(2)]
        s_o = [sem(f"o_evacuated_{L}") for L in range(2)]
        s_ot = [sem(f"o_tokens_psum_{L}") for L in range(2)]
        s_y = [sem(f"o_normalised_{L}") for L in range(2)]
        s_z = sem("gated")
        s_zp, s_zt = sem("gatedT_psum"), sem("gatedT")
        s_wo = sem("wo_psum")
        s_xb = sem("x_plus_b2")
        s_h, s_hr = sem("ffn0_hidden_psum"), sem("ffn0_hidden")
        s_f = sem("ffn0_psum")
        s_gu, s_gs, s_ga, s_hg = sem("gate_up_psum"), sem("gate_up"), sem("gate_part"), sem("ffn1_hidden")
        s_zo = sem("zero_and_one")
        s_dn = sem("ffn1_psum")
        s_xo = sem("x_final")

        block = ctx.enter_context(nc.Block())

        def at(per, b, k):
            return b * per + k

        def xt_(b):
            return xs[:, bass.ds(b * TPB, TPB), :]

        def va_(b):
            return VA[:, bass.ds(b * TPB, TPB), :]

        def pairs(eng, body):
            body(0, True, False)
            with eng.Fori(1, B // 2 - 1) as i:
                body(i, False, False)
            body(B // 2 - 1, False, True)

        def phases(eng, phase):
            def body(i, first, last):
                phase(2 * i, 0, True, not first)
                phase(2 * i + 1, 1, not last, True)
            pairs(eng, body)

        @block.sync
        def _(sp):
            x_tiles = x.rearrange("b (t p) d -> p (b t) d", p=P)
            sp.dma_start(xs[:, 0:2 * TPB], x_tiles[:, 0:2 * TPB]).then_inc(s_x, 16)
            sp.dma_start(IDF[:, :], ident).then_inc(s_id, 16)
            sp.dma_start(W0[:, 0:5 * D], w0[:, 0:5 * D]).then_inc(s_w, 16)
            sp.dma_start(TAB[:, :, :], tab).then_inc(s_tab, 16)
            sp.dma_start(xs[:, 2 * TPB:], x_tiles[:, 2 * TPB:]).then_inc(s_xr, 16)
            sp.dma_start(W0[:, 5 * D:], w0[:, 5 * D:]).then_inc(s_c, 16)
            sp.dma_start(MSF[:, :, :], masks).then_inc(s_c, 16)
            sp.dma_start(SM[:, :], small).then_inc(s_c, 16)
            sp.dma_start(W1[:, :], w1).then_inc(s_w1, 16)
            sp.dma_start(WI[:, :], wint).then_inc(s_wi, 16)

            def load_stack(L, b, p, c):
                R = NS[L] * HD
                h = R // 2
                cs = slice(HC * c, HC * (c + 1))
                sq, sk = [scr[L][bass.ds(b, 1), n].rearrange("o s (d h) t -> (o s d) h t", h=H) for n in range(2)]
                for dst, src in ((QS[L][p][0:R, cs], sq[:, cs]), (QS[L][p][R:R + h, cs], sq[0:h, cs]),
                                 (KS[L][p][0:h, cs], sk[0:h, cs]), (KS[L][p][h:h + R, cs], sk[:, cs])):
                    sp.dma_start(dst, src).then_inc(s_st[L][c], 16)

            def first_stack(L, b, stored):
                sp.wait_ge(s_init[L][b], 4 if L else 2)
                sp.wait_ge(s_ones[L], (1 + L) * (b + 1))
                sp.wait_ge(s_scr[L][b], stored)
                for c in range(2):
                    if b == 1:
                        sp.wait_ge(s_st[L][c], 64)
                    load_stack(L, b, b, c)

            def store_parts(i, first, last):
                for p in range(2):
                    b = 2 * i + p
                    for n in range(2):
                        for lo in s_lo[n:2 * n + 1]:
                            sp.wait_ge(lo, at(1, b, 1))
                        sp.dma_start(scr[0][bass.ds(b, 1), n].rearrange("o s f t -> f (o s) t"),
                                     PR[p][:, n]).then_inc(s_scr[0][p], 16)
                if first:
                    first_stack(0, 0, 32)
                if last:
                    first_stack(0, 1, 16 * B)
            pairs(sp, store_parts)

            def load_max(L, b, p, c):
                sp.wait_ge(s_ms[L], at(2, b, c + 1))
                for n in range(2):
                    sp.dma_start(QS[L][p][MROW + n:MROW + n + 1, HC * c:HC * (c + 1), :],
                                 MT[p][c][:, n, :]).then_inc(s_mi[L][c], 16)

            def store1(b, p):
                sp.wait_ge(s_lo1, at(1, b, 1))
                for n in range(2):
                    sp.dma_start(scr[1][bass.ds(b, 1), n].rearrange("o s f t -> f (o s) t"),
                                 PR1[p][:, n]).then_inc(s_scr[1][p], 16)

            def store_out(b, p):
                sp.wait_ge(s_xo, at(1, b, 1))
                sp.dma_start(out[bass.ds(b, 1)].rearrange("o (t p) d -> p (o t) d", p=P), xt_(b)).then_inc(s_out, 16)

            for L in range(2):
                def phase(b, p, scores, tail, more=True):
                    load_max(L, b, p, 1)
                    if more:
                        sp.wait_ge(s_t[L], at(16, b, HC))
                        load_stack(L, b + 2, p, 0)
                    if scores:
                        load_max(L, b + 1, 1 - p, 0)
                    if L == 0 and not (isinstance(b, int) and b < 2):
                        store1(b - 2, p)
                    if L == 1 and isinstance(b, int) and b == 0:
                        store1(B - 1, 1)
                    if L == 1 and not (isinstance(b, int) and b < 2):
                        store_out(b - 2, p)
                    if more:
                        sp.wait_ge(s_t[L], at(16, b, H))
                        load_stack(L, b + 2, p, 1)

                if L == 0:
                    load_max(0, 0, 0, 0)
                phase(0, 0, True, False)
                if L == 1:
                    for q in range(2):
                        sp.wait_ge(s_scr[1][q], 16 * B)
                phase(1, 1, True, True)
                with sp.Fori(1, B // 2 - 1) as i:
                    phase(2 * i, 0, True, True)
                    phase(2 * i + 1, 1, True, True)
                if L == 0:
                    first_stack(1, 0, 64)
                phase(B - 2, 0, True, True, more=False)
                if L == 0:
                    first_stack(1, 1, 64)
                phase(B - 1, 1, False, True, more=False)
                if L == 0:
                    load_max(1, 0, 0, 0)
                if L == 0:
                    store1(B - 2, 0)
                else:
                    for b in range(B - 2, B):
                        store_out(b, b % 2)
            sp.wait_ge(s_out, 16 * B)

        @block.gpsimd
        def _(pool):
            pool.memset(EPSC[:, 0], EPS).then_inc(s_pool, 1)
            pool.memset(EPSC[:, 1], -0.5).then_inc(s_pool, 1)
            pool.memset(EPSC[:, 2], -1.0).then_inc(s_pool, 1)

            def ones_0(p):
                pool.memset(KS[0][p][MROW:P].bitcast(U32), TWO_ONES).then_inc(s_ones[0], 1)
                pool.wait_ge(s_ones[0], p + 1)
            pool.wait_ge(s_pool, 3)
            ones_0(0)

            def rstd(n, b, p):
                chain = s_rstd[n]
                pool.wait_ge(s_var[n], at(1, b, 1))
                k = 4 if n == 3 else 2
                pool.tensor_tensor(VE[:, n, p], MV[:, n, p, :, 1], EPSC[:, 0], ALU.add).then_inc(chain, 1)
                if n == 3:
                    pool.tensor_tensor(NMN[:, p], MV[:, n, p, :, 0], EPSC[:, 2], ALU.mult).then_inc(chain, 1)
                pool.wait_ge(chain, at(k, b, k // 2))
                pool.tensor_tensor(RS[:, n, p], VE[:, n, p], EPSC[:, 1], ALU.pow).then_inc(chain, 1)
                if n == 3:
                    pool.wait_ge(chain, at(k, b, 3))
                    pool.tensor_tensor(NRS[:, p], NMN[:, p], RS[:, n, p], ALU.mult).then_inc(chain, 1)

            def rotate(b, p, first):
                if not first:
                    pool.wait_ge(s_lo[1], at(1, b, -1))
                for n in range(2):
                    pool.wait_ge(s_mul, at(2, b, n + 1))
                    pool.tensor_tensor(QR[p][:, n, 0], TQ[p][:, n, 0:S], TQ[p][:, n, S:2 * S],
                                       ALU.add).then_inc(s_rot, 1)

            def lo_k(b, p):
                pool.wait_ge(s_hi, at(2, b, 2))
                pool.tensor_tensor(PR[p][:, 1, 2], QR[p][:, 1, 0], PR[p][:, 1, 0], ALU.subtract).then_inc(s_lo[1], 1)

            def stage_a(i, first, last):
                for p in range(2):
                    b = 2 * i + p
                    if not last:
                        rstd(0, b + 2, p)
                    rotate(b, p, first)
                    if not (first and p == 0):
                        lo_k(b - 1, 1 - p)
            for p in range(2):
                rstd(0, p, p)
            pairs(pool, stage_a)
            lo_k(B - 1, 1)
            pool.wait_ge(s_lo[1], B)
            ones_0(1)
            pool.wait_ge(s_vz, 2)
            for p in range(2):
                for e in range(2):
                    ones = VP[p][:, :, :].rearrange("q t (c f r) -> q (t c) f r", f=2, r=32)[:, :, e, 16 + e:17 + e]
                    pool.memset(ones, 1.0).then_inc(s_pool, 1)
            pool.wait_ge(s_pool, 7)

            def clear_ones(p, n):
                cs = slice(HC * n, HC * (n + 1))
                pool.memset(KS[1][p][MROW:P, cs].bitcast(U32), TWO_ONES).then_inc(s_ones[1], 1)
                pool.wait_ge(s_ones[1], 2 * p + n + 1)

            def spread_v(L, b, p):
                pool.wait_ge(s_va[L], at(1, b, 1))
                dst = VP[p][:, :, :].rearrange("q t (c r) -> q t c r", r=64)
                for e in range(2):
                    ins = pool.tensor_copy(dst[:, :, :, 40 * e:40 * e + 8],
                                           va_(b).rearrange("q t (c f d) -> q t c f d", f=2, d=HD)[:, :, :, e])
                ins.then_inc(s_vp[L], 1)

            def cut(b, p, s):
                pool.wait_ge(s_e[0], at(16, b, s + 1))
                pool.tensor_tensor(HELD[:, s:s + 1], EPSC[:, 0, 0:1], EPSC[:, 0, 0:1], ALU.add)
                pr = PB[s % RING][:, :].rearrange("q (n k) -> q n k", n=2)[:, :, 0:P]
                pool.affine_select(out=pr, in_=pr, compare_op=ALU.is_ge, fill=0.0, base=0, pattern=[[0, 2], [1, P]],
                                   channel_multiplier=-1).then_inc(s_cut, 1)

            def tail_a(c, p, s):
                if s == 2:
                    pool.wait_ge(s_y[0], at(1, c, 1))
                    gb = gate_row.rearrange("q (o d) -> q o d", o=1).to_broadcast([P, TPB, D])
                    yv = Y[p][:, :].rearrange("q (t d) -> q t d", t=TPB)
                    pool.tensor_tensor(ZG[p][:, :].rearrange("q (t d) -> q t d", t=TPB), yv, gb, ALU.mult).then_inc(s_z, 1)
                if s == 9:
                    rstd(1, c, p)
                if s == 12:
                    pool.wait_ge(s_xn[1], at(1, c, 1))
                    b2 = b2_row.rearrange("q (o d) -> q o d", o=1).to_broadcast([P, TPB, D])
                    pool.tensor_tensor(xt_(c), xt_(c), b2, ALU.add).then_inc(s_xb, 1)

            def tail_b(c, p, s):
                if s == 8:
                    rstd(2, c, p)

            def tail_e(c, p, s):
                if s == 2:
                    pool.wait_ge(s_y[1], at(1, c, 1))
                    pool.tensor_tensor(xt_(c), xt_(c), Y[p][:, :].rearrange("q (t d) -> q t d", t=TPB),
                                       ALU.add).then_inc(s_res[2], 1)
                if s == 3:
                    rstd(3, c, p)
                if s - 1 in GU and not (isinstance(c, int) and c == B - 1):
                    j = GU.index(s - 1)
                    pool.wait_ge(s_gs, at(3, c, j + 1))
                    if j or not (isinstance(c, int) and c == 0):
                        pool.wait_ge(s_ga, at(6, c, 2 * j))
                    pool.tensor_tensor(GA[0][:, :], TH[j][:, :], GS[j][:, 0:S], ALU.mult).then_inc(s_ga, 1)
                    pool.wait_ge(s_ga, at(6, c, 2 * j + 1))
                    if j or not (isinstance(c, int) and c == 0):
                        pool.wait_ge(s_hg, at(3, c, j))
                    pool.tensor_tensor(GA[1][:, :], GA[0][:, :], GS[j][:, 0:S], ALU.add).then_inc(s_ga, 1)

            def tails(L, b, p, s):
                if L == 0:
                    if not (isinstance(b, int) and b < 1):
                        tail_a(b - 1, 1 - p, s)
                    if not (isinstance(b, int) and b < 2):
                        tail_b(b - 2, p, s)
                elif isinstance(b, int) and b == 0:
                    tail_b(B - 1, 1, s)
                else:
                    tail_e(b - 1, 1 - p, s)

            for b in range(2):
                spread_v(0, b, b)
            for L in range(2):
                def phase(b, p, scores, later):
                    for s in range(H):
                        if L == 0:
                            cut(b, p, s)
                            if isinstance(b, int) and b < 2 and s in (4, 10):
                                pool.wait_ge(s_cut, at(16, b, s + 1))
                                clear_ones(b, s // 10)
                        if later and scores and s == 6:
                            pool.wait_ge(s_pv[L], at(4, b, 0))
                            spread_v(L, b + 1, 1 - p)
                        tails(L, b, p, s)
                phases(pool, phase)
                for s in range(H):
                    if L == 0 and s == 3:
                        pool.wait_ge(s_pv[0], 4 * B)
                        for b in range(2):
                            spread_v(1, b, b)
                    tails(L, B, 0, s)

        @block.scalar
        def _(act):
            act.wait_ge(s_zo, 2)

            def fill(dst, k):
                shape = list(dst.shape)
                src = ZO[0:shape[0], k:k + 1]
                return act.copy(dst, src.to_broadcast(shape))

            def clear_0(p):
                fill(QS[0][p][:, :, :].rearrange("q h t -> q (h t)").bitcast(F32), 0).then_inc(s_init[0][p], 1)
                fill(KS[0][p][0:MROW].rearrange("q h t -> q (h t)").bitcast(F32), 0).then_inc(s_init[0][p], 1)
            clear_0(0)

            def copy_xt(b, p):
                act.wait_ge(s_xtp[0], at(1, b, 1))
                act.copy(XT[0][p][:, :], bank[p][:, 0:S]).then_inc(s_xt[0], 1)

            def stage_a(i, first, last):
                for p in range(2):
                    b = 2 * i + p
                    if not (last and p == 1):
                        copy_xt(b + 1, 1 - p)
                    for n in range(2):
                        act.wait_ge(s_rot, at(2, b, n + 1))
                        act.activation(QR[p][:, n, 1], QR[p][:, n, 0], ACT.Square,
                                       scale=float(np.sqrt(LAM / QSCALE)) if n == 0 else 1.0).then_inc(s_act, 1)
                    act.wait_ge(s_v[0], at(1, b, 1))
                    act.copy(va_(b), bank[4 + 3 * p][:, 0:S].rearrange("q (t d) -> q t d", t=TPB)).then_inc(s_va[0], 1)
                    if not first:
                        act.wait_ge(s_scr[0][p], 32 * i)
                    for n in range(2):
                        act.wait_ge(s_act, at(2, b, n + 1))
                        act.copy(PR[p][:, n, 0:2], QR[p][:, n]).then_inc(s_hi, 1)
                if first:
                    for q in range(2):
                        fill(VP[q][:, :, :].rearrange("q t c -> q (t c)"), 0).then_inc(s_vz, 1)
            copy_xt(0, 0)
            pairs(act, stage_a)
            clear_0(1)

            def exp(L, b, p, s):
                act.wait_ge(s_t[L], at(16, b, s + 1))
                if not (isinstance(b, int) and 4 * b + s // 4 - 1 <= 0):
                    act.wait_ge(s_pv[L], at(4, b, s // 4 - 1))
                n = 384 if L == 0 else 512
                act.activation(PB[s % RING][:, 0:n], TB_[s % 2][:, 0:n], ACT.Exp).then_inc(s_e[L], 1)

            def hi_max(L, b, p, c):
                act.wait_ge(s_mt[L], at(2, b, c + 1))
                act.copy(MT[p][c][:, 0], MISC[1][0:HC, 0:S]).then_inc(s_mh[L], 1)

            def normalise(b, p):
                act.wait_ge(s_rstd[3], at(4, b, 4))
                act.copy(HOLDA[:, p:p + 1], ZO[:, 0:1])
                for t in range(TPB):
                    ins = act.activation(XN[3][p][:, t], xs[:, b * TPB + t], ACT.Identity, bias=NRS[:, p, t:t + 1],
                                         scale=RS[:, 3, p, t:t + 1])
                ins.then_inc(s_xn[3], 1)

            def evac_o(L, b, p, c):
                act.wait_ge(s_pv[L], at(4, b, 2 * c + 2))
                act.copy(OT[p][c][:, :], VB_[:, 0:S]).then_inc(s_o[L], 1)

            def tail_a(c, p, s):
                if s == 5:
                    act.wait_ge(s_zp, at(1, c, 1))
                    act.copy(ZT[p][:, :], MISC[1][:, 0:S]).then_inc(s_zt, 1)
                if s == 14:
                    act.wait_ge(s_xtp[1], at(1, c, 1))
                    act.copy(XT[1][p][:, :], MISC[1][:, 0:S]).then_inc(s_xt[1], 1)

            def tail_b(c, p, s):
                if s in (3, 4):
                    k = s - 3
                    act.wait_ge(s_h, at(2, c, k + 1))
                    for j in range(2):
                        ins = act.activation(HR[p][:, 2 * k + j], MISC[1 - k][:, j * S:(j + 1) * S], ACT.Relu,
                                             bias=b1_col[:, 2 * k + j:2 * k + j + 1])
                    ins.then_inc(s_hr, 1)
                if s == 12:
                    act.wait_ge(s_xtp[2], at(1, c, 1))
                    act.activation(XT[2][p][:, :], MISC[0][:, 0:S], ACT.Identity, bias=b_col,
                                   scale=g_col).then_inc(s_xt[2], 1)
                if s == 14:
                    act.wait_ge(s_qk1, at(1, c, 1))
                    act.activation(QR1[p][:, 0], MISC[0][:, 0:S], ACT.Identity, bias=bqs_col, scale=QSCALE)
                    act.activation(QR1[p][:, 1], MISC[0][:, S:2 * S], ACT.Identity, bias=bk_col).then_inc(s_qr1, 1)
                    act.wait_ge(s_qr1, at(1, c, 1))
                    if not (isinstance(c, int) and c < 2):
                        act.wait_ge(s_scr[1][p], at(16, c, -16 * p))
                    act.copy(PR1[p][:, :, 0], QR1[p][:, :, :]).then_inc(s_hi1, 1)

            def tail_e(c, p, s):
                if s == 6:
                    normalise(c, p)
                if s == 9:
                    act.wait_ge(s_xtp[3], at(1, c, 1))
                    act.copy(XHL[p][:, 0], MISC[1][:, 0:S]).then_inc(s_xt[3], 1)
                if s in GU:
                    j = GU.index(s)
                    act.wait_ge(s_gu, at(3, c, j + 1))
                    act.activation(TH[j][:, :], MISC[j % 2][:, 0:S], ACT.Tanh, scale=0.5 * SCALE)
                    act.mul(GS[j][:, :], MISC[j % 2][:, :], SCALE * float(np.sqrt(0.5))).then_inc(s_gs, 1)

            def tails(L, b, p, s):
                if L == 0:
                    if not (isinstance(b, int) and b < 1):
                        tail_a(b - 1, 1 - p, s)
                    if not (isinstance(b, int) and b < 2):
                        tail_b(b - 2, p, s)
                elif isinstance(b, int) and b == 0:
                    tail_b(B - 1, 1, s)
                else:
                    tail_e(b - 1, 1 - p, s)

            hi_max(0, 0, 0, 0)
            for L in range(2):
                if L == 1:
                    act.wait_ge(s_pv[0], 4 * B)

                def phase(b, p, scores, later):
                    for s in range(H):
                        exp(L, b, p, s)
                        if L == 0 and isinstance(b, int) and b == 1 and s == 0:
                            act.wait_ge(s_prep, 2)
                        if L == 0 and isinstance(b, int) and b < 2 and s in (6, 12):
                            cs = slice(HC * (s // 12), HC * (s // 12 + 1))
                            fill(KS[1][b][0:MROW, cs].rearrange("q h t -> q (h t)").bitcast(F32), 0).then_inc(s_init[1][b], 1)
                        if s == 1 and later:
                            evac_o(L, b - 1, 1 - p, 1)
                        if s == M1[L]:
                            hi_max(L, b, p, 1)
                        if s == M0[L] and scores:
                            hi_max(L, b + 1, 1 - p, 0)
                        if s == 11:
                            evac_o(L, b, p, 0)
                        tails(L, b, p, s)
                phases(act, phase)
                evac_o(L, B - 1, 1, 1)
                for s in range(H):
                    if L == 0 and s == M0[0]:
                        hi_max(1, 0, 0, 0)
                    tails(L, B, 0, s)

        @block.vector
        def _(dve):
            for k in range(2):
                dve.memset(ZO[:, k:k + 1], float(k)).then_inc(s_zo, 1)
            dve.wait_ge(s_x, 16)

            def held():
                dve.memset(HOLD[:, :], 0.0)

            def variance(n, b, p, chain):
                for t in range(TPB):
                    dve.bn_stats(STAT[:, n, p, t], xs[:, b * TPB + t]).then_inc(chain, 1)
                dve.wait_ge(chain, at(TPB, b, TPB))
                held()
                for t in range(TPB):
                    ins = dve.bn_aggr(MV[:, n, p, t], STAT[:, n, p, t])
                ins.then_inc(s_var[n], 1)

            def normalise(n, b, p):
                dve.wait_ge(s_rstd[n], at(2, b, 2))
                for t in range(TPB):
                    ins = dve.tensor_scalar(XN[n][p][:, t], xs[:, b * TPB + t], MV[:, n, p, t, 0:1], RS[:, n, p, t:t + 1],
                                            ALU.subtract, ALU.mult)
                ins.then_inc(s_xn[n], 1)

            def products(b, p):
                for n in range(2):
                    dve.wait_ge(s_qk, at(2, b, n + 1))
                    dve.tensor_tensor(TQ[p][:, n], bank[2 + n + 3 * p][:, :], TAB[:, n], ALU.mult).then_inc(s_mul, 1)

            def lo_q(b, p):
                dve.wait_ge(s_hi, at(2, b, 1))
                dve.tensor_tensor(PR[p][:, 0, 2:4], QR[p][:, 0], PR[p][:, 0, 0:2], ALU.subtract).then_inc(s_lo[0], 1)
                dve.wait_ge(s_hi, at(2, b, 2))
                dve.tensor_tensor(PR[p][:, 1, 3], QR[p][:, 1, 1], PR[p][:, 1, 1], ALU.subtract).then_inc(s_lo[2], 1)

            def prepare():
                dve.wait_ge(s_wi, 16)
                dve.tensor_copy(WGU[:, :], WI[:, 0:2 * HIDDEN]).then_inc(s_prep, 1)
                dve.tensor_scalar(bqs_col, bq_col, QSCALE, None, ALU.mult).then_inc(s_prep, 1)
                dve.tensor_scalar(WD[:, :, :], WI[:, 2 * HIDDEN:].rearrange("p (n d) -> p n d", n=NG), SCALE, None,
                                  ALU.mult).then_inc(s_prep, 1)
                dve.tensor_scalar(gate_row, gate_row, HADAMARD, None, ALU.mult).then_inc(s_prep, 1)
                dve.wait_ge(s_prep, 4)

            def stage_a(i, first, last):
                for p in range(2):
                    b = 2 * i + p
                    if not last:
                        if first and p == 0:
                            dve.wait_ge(s_xr, 16)
                        variance(0, b + 2, p, s_stat[0])
                    products(b, p)
                    if not (first and p == 0):
                        lo_q(b - 1, 1 - p)
                    if not last:
                        normalise(0, b + 2, p)
                if first:
                    dve.wait_ge(s_c, 48)
                    dve.tensor_copy(MSK[:, :, :], MSF[:, :, :]).then_inc(s_msk, 1)
            for p in range(2):
                variance(0, p, p, s_stat[0])
            for p in range(2):
                normalise(0, p, p)
            dve.wait_ge(s_tab, 16)
            pairs(dve, stage_a)
            lo_q(B - 1, 1)

            def maximum(L, b, p, s):
                n = 3 if L == 0 else 2
                dve.wait_ge(s_s[L], at(16, b, s + 1))
                w = 384 if L == 0 else 512
                dve.tensor_reduce(NM[p][:, s, 0:n], SB_[score_bank(s)][:, 0:w].rearrange("q (n k) -> q n k", n=n),
                                  AX.X, ALU.max, negate=True).then_inc(s_mx[L], 1)
                if L == 0 and s % HC == HC - 1:
                    dve.wait_ge(s_mx[L], at(16, b, s + 1))
                    cs = slice(s + 1 - HC, s + 1)
                    dve.tensor_tensor(NMB[p][:, cs], NM[p][:, cs, 1], NM[p][:, cs, 2], ALU.min).then_inc(s_mb, 1)

            def lo_max(L, b, p, c):
                dve.wait_ge(s_mh[L], at(2, b, c + 1))
                dve.tensor_tensor(MT[p][c][:, 1], MISC[1][0:HC, 0:S], MT[p][c][:, 0], ALU.subtract).then_inc(s_ms[L], 1)

            def norm_o(L, c, p):
                o = MISC[0][:, :].rearrange("q (n r) -> q n r", r=32)
                dve.wait_ge(s_ot[L], at(1, c, 1))
                dve.reciprocal(REC[p][:, :, :], o[:, :, 16:18]).then_inc(s_rec[L], 1)
                dve.wait_ge(s_rec[L], at(1, c, 1))
                dve.tensor_tensor(Y[p][:, :].rearrange("q (n e d) -> q n e d", e=2, d=HD),
                                  o[:, :, 0:16].rearrange("q n (e d) -> q n e d", e=2),
                                  REC[p][:, :, :].rearrange("q n (e o) -> q n e o", o=1).to_broadcast([P, 16, 2, HD]),
                                  ALU.mult).then_inc(s_y[L], 1)

            def add_stream(c, other, done):
                dve.tensor_tensor(xt_(c), xt_(c), other, ALU.add).then_inc(done, 1)
                dve.wait_ge(done, at(1, c, 1))
                held()

            m0, m1 = [m[:, 0:S].rearrange("q (t d) -> q t d", t=TPB) for m in MISC]

            def tail_a(c, p, s):
                if s == 2:
                    norm_o(0, c, p)
                if s == 4:
                    dve.wait_ge(s_z, at(2, c, 1))
                    dve.scalar_tensor_tensor(out=Z[p][:, :], in0=ZG[p][:, :], scalar=1.0, in1=Y[p][:, :],
                                             op0=ALU.add, op1=ALU.mult).then_inc(s_z, 1)
                if s == 8:
                    dve.wait_ge(s_wo, at(1, c, 1))
                    add_stream(c, m1, s_res[0])
                    variance(1, c, p, s_stat[1])

                if s == 12:
                    normalise(1, c, p)

            def tail_b(c, p, s):
                if s == 7:
                    dve.wait_ge(s_f, at(1, c, 1))
                    dve.wait_ge(s_xb, at(1, c, 1))
                    add_stream(c, m0, s_res[1])
                    variance(2, c, p, s_stat[2])
                if s == 10:
                    normalise(2, c, p)
                if s == 15:
                    dve.wait_ge(s_hi1, at(1, c, 1))
                    dve.tensor_tensor(PR1[p][:, :, 1], QR1[p][:, :, :], PR1[p][:, :, 0], ALU.subtract).then_inc(s_lo1, 1)
                    dve.wait_ge(s_v[1], at(1, c, 1))
                    bv = bv_row.rearrange("q (o d) -> q o d", o=1).to_broadcast([P, TPB, D])
                    dve.tensor_tensor(va_(c), MISC[1][:, 0:S].rearrange("q (t d) -> q t d", t=TPB), bv,
                                      ALU.add).then_inc(s_va[1], 1)

            def tail_e(c, p, s):
                if s == 2:
                    norm_o(1, c, p)
                if s == 3:
                    dve.wait_ge(s_res[2], at(1, c, 1))
                    held()
                    variance(3, c, p, s_stat[3])
                if s == 9:
                    dve.wait_ge(s_xt[3], at(1, c, 1))
                    dve.tensor_tensor(XHL[p][:, 1], MISC[1][:, 0:S], XHL[p][:, 0], ALU.subtract).then_inc(s_xlo, 1)
                if s in (13, 15):
                    hidden(c, p, s // 2 - 6)

            def hidden(c, p, j):
                if isinstance(c, int) and c == B - 1:
                    dve.wait_ge(s_gs, at(3, c, j + 1))
                    dve.wait_ge(s_hg, at(3, c, j))
                    dve.scalar_tensor_tensor(out=GA[1][:, :], in0=TH[j][:, :], scalar=1.0, in1=GS[j][:, 0:S],
                                             op0=ALU.add, op1=ALU.mult).then_inc(s_ga, 1)
                    dve.wait_ge(s_ga, at(6, c, j + 1))
                else:
                    dve.wait_ge(s_ga, at(6, c, 2 * j + 2))
                dve.tensor_tensor(HG[p][:, j], GA[1][:, :], GS[j][:, S:2 * S], ALU.mult).then_inc(s_hg, 1)

            def tail_f(c, p, s):
                if s == 0:
                    hidden(c, p, 2)
                if s == 3:
                    dve.wait_ge(s_dn, at(1, c, 1))
                    dve.tensor_tensor(xt_(c), xt_(c), m1, ALU.add).then_inc(s_xo, 1)

            def tails(L, b, p, s):
                if L == 0:
                    if not (isinstance(b, int) and b < 1):
                        tail_a(b - 1, 1 - p, s)
                    if not (isinstance(b, int) and b < 2):
                        tail_b(b - 2, p, s)
                elif isinstance(b, int) and b == 0:
                    tail_b(B - 1, 1, s)
                else:
                    if not (isinstance(b, int) and b < 2):
                        tail_f(b - 2, p, s)
                    tail_e(b - 1, 1 - p, s)

            for s in range(H):
                maximum(0, 0, 0, s)
                if s == M0[0] + 1:
                    lo_max(0, 0, 0, 0)
            for L in range(2):
                def phase(b, p, scores, later):
                    for s in range(H):
                        if scores:
                            maximum(L, b + 1, 1 - p, s)
                        if L == 0 and isinstance(b, int) and b == 0 and s == 2:
                            prepare()
                        if L == 0 and isinstance(b, int) and b < 2 and s in (6, 12):
                            cs = slice(HC * (s // 12), HC * (s // 12 + 1))
                            dve.memset(QS[1][b][:, cs].bitcast(U32), 0).then_inc(s_init[1][b], 1)
                        if s == M1[L] + 1:
                            lo_max(L, b, p, 1)
                        if scores and s == M0[L] + 1:
                            lo_max(L, b + 1, 1 - p, 0)
                        tails(L, b, p, s)
                phases(dve, phase)
                for s in range(H):
                    if L == 0:
                        maximum(1, 0, 0, s)
                        if s == M0[0] + 1:
                            lo_max(1, 0, 0, 0)
                    tails(L, B, 0, s)
            for s in (0, 3):
                tail_f(B - 1, 1, s)

        @block.tensor
        def _(pe):
            def norm_t(n, b, p, dst):
                pe.wait_ge(s_xn[n], at(1, b, 1))
                for t in range(TPB):
                    ins = pe.transpose(dst[:, t * P:(t + 1) * P], XN[n][p][:, t], IDF[:, :])
                ins.then_inc(s_xtp[n], 1)

            def project(b, p, first):
                xt = XT[0][p]
                pe.wait_ge(s_xt[0], at(1, b, 1))
                if not first:
                    pe.wait_ge(s_mul, at(2, b, -2))
                    pe.wait_ge(s_va[0], at(1, b, -1))
                for n, (w, wr) in enumerate(((wq, wrq), (wk, wrk))):
                    pe.matmul(bank[2 + n + 3 * p][:, 0:S], w, xt[:, :], start=True, stop=True)
                    pe.matmul(bank[2 + n + 3 * p][:, S:2 * S], wr, xt[:, :], start=True, stop=True).then_inc(s_qk, 1)

            def project_v(b, p):
                xt = XT[0][p]
                for t in range(TPB):
                    ins = pe.matmul(bank[4 + 3 * p][:, t * D:(t + 1) * D], xt[:, t * P:(t + 1) * P], wv,
                                    start=True, stop=True)
                ins.then_inc(s_v[0], 1)

            def stage_a(i, first, last):
                for p in range(2):
                    b = 2 * i + p
                    project(b, p, first)
                    if not (last and p == 1):
                        norm_t(0, b + 1, 1 - p, bank[1 - p])
                    project_v(b, p)
            pe.wait_ge(s_id, 16)
            norm_t(0, 0, 0, bank[0])
            pe.wait_ge(s_w, 16)
            pairs(pe, stage_a)

            pe.wait_ge(s_c, 48)
            pe.wait_ge(s_mul, 2 * B - 2)
            pe.wait_ge(s_va[0], B - 1)
            pe.wait_ge(s_msk, 1)

            def scores(L, b, p, s):
                if s % HC == 0:
                    pe.wait_ge(s_st[L][s // HC], at(64, b, 64))
                if bank_free(s) > 0 or not (isinstance(b, int) and b == 0):
                    pe.wait_ge(s_mx[L], at(16, b, bank_free(s)))
                q, k, o = QS[L][p][0:MROW, s], KS[L][p][0:MROW, s], SB_[score_bank(s)]
                if L == 0:
                    pe.matmul(o[:, 0:P], MSK[:, 0], MSK[:, 1], start=True, stop=True)
                    pe.matmul(o[:, 0:P], q[:, 0:P], k[:, 0:P], start=False, stop=True, skip_group_check=True)
                    pe.matmul(o[:, 2 * P:3 * P], MSK[:, 0], MSK[:, 1], start=True, stop=True, skip_group_check=True)
                    ins = pe.matmul(o[:, P:3 * P], q[:, P:2 * P], k[:, :], start=False, stop=True,
                                    skip_group_check=True)
                else:
                    pe.matmul(o[:, 0:S], q[:, 0:P], k[:, :], start=True, stop=True)
                    ins = pe.matmul(o[:, S:2 * S], q[:, P:2 * P], k[:, :], start=True, stop=True)
                ins.then_inc(s_s[L], 1)

            def max_rows(L, b, p, c):
                if L == 0:
                    pe.wait_ge(s_mb, at(2, b, c + 1))
                else:
                    pe.wait_ge(s_mx[L], at(16, b, HC * (c + 1)))
                if c == 1 or not (isinstance(b, int) and b == 0):
                    pe.wait_ge(s_ms[L], at(2, b, c))
                cs = slice(HC * c, HC * (c + 1))
                m = MISC[1]
                pe.transpose(m[0:HC, 0:P], NM[p][:, cs, 0], IDF[:, :])
                pe.transpose(m[0:HC, P:2 * P], NMB[p][:, cs] if L == 0 else NM[p][:, cs, 1],
                             IDF[:, :]).then_inc(s_mt[L], 1)

            def shifted(L, b, p, s):
                if s % HC == 0:
                    pe.wait_ge(s_mi[L][s // HC], at(32, b, 32))
                if s >= 2 or not (isinstance(b, int) and b == 0):
                    pe.wait_ge(s_e[L], at(16, b, s - 1))
                q, k, o = QS[L][p][:, s], KS[L][p][:, s], TB_[s % 2]
                pe.matmul(o[:, 0:S], k[:, 0:P], q[:, :], start=True, stop=True)
                if L == 0:
                    ins = pe.matmul(o[:, S:S + P], k[:, P:2 * P], q[:, P:2 * P], start=True, stop=True)
                else:
                    ins = pe.matmul(o[:, S:2 * S], k[:, P:2 * P], q[:, :], start=True, stop=True)
                ins.then_inc(s_t[L], 1)

            def pv(L, b, p, g):
                pe.wait_ge(s_cut if L == 0 else s_e[1], at(16, b, 4 * g + 4))
                if g == 0:
                    pe.wait_ge(s_vp[L], at(1, b, 1))
                if g % 2 == 0 and not (isinstance(b, int) and 2 * b + g // 2 == 0):
                    pe.wait_ge(s_o[L], at(2, b, g // 2))
                for kt in range(TPB):
                    for j in range(4):
                        s = 4 * g + j
                        v = VP[p][:, kt, 32 * (8 * (g // 2) + 2 * j + g % 2):][:, 0:32]
                        pr = PB[s % RING]
                        if L == 0 and kt == 1:
                            o, pr = VB_[32 * j:32 * j + 32, P:S], pr[:, S:S + P]
                        else:
                            o, pr = VB_[32 * j:32 * j + 32, 0:S], pr[:, kt * S:(kt + 1) * S]
                        ins = pe.matmul(o, v, pr, start=(g % 2 == 0 and kt == 0), stop=True, skip_group_check=True)
                ins.then_inc(s_pv[L], 1)

            def turn_o(L, c, p):
                pe.wait_ge(s_o[L], at(2, c, 2))
                if L == 1 and not (isinstance(c, int) and c == 0):
                    pe.wait_ge(s_gs, at(3, c, 0))
                for t in range(TPB):
                    for k in range(2):
                        ins = pe.transpose(MISC[0][:, (2 * t + k) * P:(2 * t + k + 1) * P],
                                           OT[p][k][:, t * P:(t + 1) * P], IDF[:, :])
                ins.then_inc(s_ot[L], 1)

            def tail_a(c, p, s, free1, free2):
                if s == 2:
                    turn_o(0, c, p)
                if s == 5:
                    pe.wait_ge(s_z, at(2, c, 2))
                    pe.wait_ge(*free1)
                    for t in range(TPB):
                        ins = pe.transpose(MISC[1][:, t * P:(t + 1) * P], Z[p][:, t * D:(t + 1) * D], IDF[:, :])
                    ins.then_inc(s_zp, 1)
                if s == 7:
                    pe.wait_ge(s_zt, at(1, c, 1))
                    for t in range(TPB):
                        ins = pe.matmul(MISC[1][:, t * D:(t + 1) * D], ZT[p][:, t * P:(t + 1) * P], wo,
                                        start=True, stop=True)
                    ins.then_inc(s_wo, 1)
                if s == 14:
                    pe.wait_ge(s_var[1], at(1, c, 1))
                    if free2 is not None:
                        pe.wait_ge(*free2)
                    norm_t(1, c, p, MISC[1])

            def tail_b(c, p, s, free1, free0, free2):
                if s in (3, 4):
                    k = s - 3
                    if k == 0:
                        pe.wait_ge(s_xt[1], at(1, c, 1))
                        pe.wait_ge(*free1)
                    else:
                        pe.wait_ge(*free0)
                    for j in range(2):
                        n = 2 * k + j
                        ins = pe.matmul(MISC[1 - k][:, j * S:(j + 1) * S], wi1[:, n * P:(n + 1) * P], XT[1][p][:, :],
                                        start=True, stop=True)
                    ins.then_inc(s_h, 1)
                if s == 6:
                    pe.wait_ge(s_hr, at(2, c, 2))
                    for t in range(TPB):
                        for n in range(NI):
                            ins = pe.matmul(MISC[0][:, t * D:(t + 1) * D], HR[p][:, n, t * P:(t + 1) * P], wi2[:, n],
                                            start=(n == 0), stop=(n == NI - 1))
                    ins.then_inc(s_f, 1)
                if s == 12:
                    pe.wait_ge(s_var[2], at(1, c, 1))
                    norm_t(2, c, p, MISC[0])
                if s == 14:
                    pe.wait_ge(s_xt[2], at(1, c, 1))
                    for n in range(2):
                        ins = pe.matmul(MISC[0][:, n * S:(n + 1) * S], W1[:, n * D:(n + 1) * D], XT[2][p][:, :],
                                        start=True, stop=True)
                    ins.then_inc(s_qk1, 1)
                if s == 15:
                    pe.wait_ge(*free2)
                    for t in range(TPB):
                        ins = pe.matmul(MISC[1][:, t * D:(t + 1) * D], XT[2][p][:, t * P:(t + 1) * P], W1[:, 2 * D:3 * D],
                                        start=True, stop=True)
                    ins.then_inc(s_v[1], 1)

            def tail_e(c, p, s, free1, free2):
                if s == 2:
                    turn_o(1, c, p)
                if s == 9:
                    if not (isinstance(c, int) and c == 0):
                        pe.wait_ge(s_xo, at(1, c, 0))
                    else:
                        pe.wait_ge(*free1)
                    norm_t(3, c, p, MISC[1])
                if s in GU:
                    j = GU.index(s)
                    if j == 0:
                        pe.wait_ge(s_y[1], at(1, c, 1))
                        pe.wait_ge(s_xlo, at(1, c, 1))
                    if j == 1 and free2 is not None:
                        pe.wait_ge(*free2)
                    if j == 2:
                        pe.wait_ge(s_gs, at(3, c, 1))
                    for n in range(2):
                        w = WGU[:, n * HIDDEN + j * P:n * HIDDEN + (j + 1) * P]
                        for k in range(2):
                            ins = pe.matmul(MISC[j % 2][:, n * S:(n + 1) * S], w, XHL[p][:, k], start=(k == 0),
                                            stop=(k == 1))
                    ins.then_inc(s_gu, 1)

            def tail_f(c, p, free1):
                if free1 is not None:
                    pe.wait_ge(*free1)
                pe.wait_ge(s_hg, at(3, c, 3))
                for t in range(TPB):
                    for n in range(NG):
                        ins = pe.matmul(MISC[1][:, t * D:(t + 1) * D], HG[p][:, n, t * P:(t + 1) * P], WD[:, n],
                                        start=(n == 0), stop=(n == NG - 1))
                ins.then_inc(s_dn, 1)

            def tails(L, b, p, s, with_scores):
                own = not (isinstance(b, int) and b == B)
                has_b = not (isinstance(b, int) and b < 2)
                m1 = (s_ms[L], at(2, b, 2)) if own else None
                m0 = ((s_ms[L], at(2, b, 3)) if own else (s_ms[1], 1)) if with_scores or (L == 0 and not own) else None
                if L == 0:
                    if has_b:
                        tail_b(b - 2, p, s, m1 or (s_va[1], B - 2), (s_y[0], at(1, b, 0)), (s_xt[1], at(1, b, 0)))
                    if not (isinstance(b, int) and b < 1):
                        tail_a(b - 1, 1 - p, s, (s_hr, at(2, b, -3)) if has_b else m1, m0)
                elif isinstance(b, int) and b == 0:
                    tail_b(B - 1, 1, s, m1, (s_qr1, B - 1), (s_ms[1], 3))
                else:
                    tail_e(b - 1, 1 - p, s, m1, m0)
                    if s == 3 and has_b:
                        tail_f(b - 2, p, m1)

            pe.wait_ge(s_w1, 16)
            for s in range(H):
                scores(0, 0, 0, s)
                if s == M0[0]:
                    pe.wait_ge(s_mul, 2 * B)
                    pe.wait_ge(s_va[0], B)
                    max_rows(0, 0, 0, 0)
            for L in range(2):
                def phase(b, p, with_scores, later):
                    for s in range(H):
                        if with_scores:
                            scores(L, b + 1, 1 - p, s)
                        shifted(L, b, p, s)
                        if s == 1 and later:
                            pv(L, b - 1, 1 - p, 3)
                        if s == M1[L]:
                            if L == 1 and isinstance(b, int) and b == 1:
                                pe.wait_ge(s_va[1], B)
                            elif L == 1 and later:
                                pe.wait_ge(s_gs, at(3, b, -3))
                            elif L == 0 and with_scores:
                                pe.wait_ge(s_mx[0], at(16, b, H + 1))
                            elif L == 0:
                                pe.wait_ge(s_va[1], at(1, b, -2))
                            max_rows(L, b, p, 1)
                        if s in PV[L]:
                            pv(L, b, p, PV[L].index(s))
                        if with_scores and s == M0[L]:
                            if later:
                                pe.wait_ge(s_res[0] if L == 0 else s_xlo, at(1, b, 0))
                            max_rows(L, b + 1, 1 - p, 0)
                        tails(L, b, p, s, with_scores)

                phases(pe, phase)
                if L == 0:
                    pe.wait_ge(s_mx[0], 16 * B)
                    pe.wait_ge(s_prep, 4)
                for s in range(H):
                    if L == 0:
                        scores(1, 0, 0, s)
                    if s == 1:
                        pv(L, B - 1, 1, 3)
                    if L == 0 and s == M0[0]:
                        pe.wait_ge(s_res[0], B)
                        max_rows(1, 0, 0, 0)
                    tails(L, B, 0, s, False)
                if L == 1:
                    tail_f(B - 1, 1, None)
                if L == 0:
                    pe.wait_ge(s_e[0], 16 * B)
                    pe.wait_ge(s_o[0], 2 * B)
                    pe.wait_ge(s_va[1], B - 1)


def _program_inputs(inputs):
    a = {k: np.asarray(v) for k, v in inputs.items()}
    heads = np.array([head_of_slot(s) for s in range(H)])
    feat = (np.arange(HD)[:, None] + HD * heads[None, :]).reshape(-1)
    rot = ((np.arange(HD)[:, None] + HD // 2) % HD + HD * heads[None, :]).reshape(-1)
    half = HD // 2
    inv = (1.0 / 10000.0 ** (np.arange(half, dtype=np.float32) / np.float32(half))).astype(np.float32)
    ang = np.arange(S, dtype=np.float32)[:, None] * inv[None, :]
    j = np.arange(P) // H
    cos = np.cos(ang).astype(np.float32).T[j % half]
    sin = np.sin(ang).astype(np.float32).T[j % half] * np.where(j < half, -1, 1).astype(np.float32)[:, None]
    qs = np.float32(QSCALE)
    tab = np.stack([np.concatenate([cos * qs, sin * qs], 1), np.concatenate([cos, sin], 1)], 1)
    c = np.ascontiguousarray
    w0 = np.concatenate([a["L0_attn_Wq"][feat].T, a["L0_attn_Wq"][rot].T, a["L0_attn_Wk"][feat].T,
                         a["L0_attn_Wk"][rot].T, a["L0_attn_Wv"].T, a["L0_attn_Wo"].T, a["L0_ffn_W1"],
                         a["L0_ffn_W2"].reshape(NI, P, D).transpose(1, 0, 2).reshape(P, NI * D)], 1)

    def rows(v):
        return np.broadcast_to(v[None, :], (P, D))

    def col(v):
        return v.reshape(-1, P).T

    small = np.concatenate([rows(np.tile(a["L0_attn_gate_w"], H)), rows(a["L0_ffn_b2"]), rows(a["L1_attn_bv"]),
                            rows(a["L1_attn_bv"]), col(a["L0_ffn_b1"]), col(a["L1_attn_ln_g"]), col(a["L1_attn_ln_b"]),
                            col(a["L1_attn_bq"][feat]), col(a["L1_attn_bk"][feat]), col(a["L1_attn_bk"][feat])], 1)
    w1 = np.concatenate([a["L1_attn_Wq"][:, feat], a["L1_attn_Wk"][:, feat], a["L1_attn_Wv"]], 1)
    wint = np.concatenate([a["L1_ffn_w_gate"].T, a["L1_ffn_w_up"].T,
                           a["L1_ffn_w_down"].T.reshape(NG, P, D).transpose(1, 0, 2).reshape(P, NG * D)], 1)
    upper = np.triu(np.ones((P, P), np.float32), 1) * np.float32(-1e30)
    masks = np.stack([np.eye(P, dtype=np.float32), upper, upper.T], 1)
    return {"x": c(a["L0_attn_x"]), "w0": c(w0), "tab": c(tab), "small": c(small), "w1": c(w1), "wint": c(wint),
            "ident": np.eye(P, dtype=np.float32), "masks": c(masks)}


def kernel(**inputs):
    from concourse import bacc
    from concourse.bass_utils import run_bass_kernel_spmd

    nc = bacc.Bacc("TRN2", target_bir_lowering=False, num_devices=1)
    arrays = _program_inputs(inputs)
    args = {n: nc.dram_tensor(f"in_{n}", v.shape, mybir.dt.from_np(v.dtype), kind="ExternalInput").ap()
            for n, v in arrays.items()}
    out = nc.dram_tensor("out_x", (B, S, D), F32, kind="ExternalOutput").ap()
    program(nc, *args.values(), out)
    r = run_bass_kernel_spmd(nc, [{f"in_{n}": v for n, v in arrays.items()}], core_ids=[0])
    return r.results[0]["out_x"]
```
